# Optimizing a Trainium2 kernel written in Bass

```python
import numpy as np
import jax
import jax.numpy as jnp

def _softmax(x, axis=-1):
    return jax.nn.softmax(x, axis=axis)

def _gelu(x):
    return jax.nn.gelu(x, approximate=True)

def _silu(x):
    return jax.nn.silu(x)

def _sigmoid(x):
    return jax.nn.sigmoid(x)

def _layernorm(x, axis=-1, eps=1e-05):
    m = jnp.mean(x, axis=axis, keepdims=True)
    v = jnp.var(x, axis=axis, keepdims=True)
    return (x - m) / jnp.sqrt(v + eps)

def _scatter_add(tgt, idx, src, axis=0):
    return tgt.at[idx].add(src)

def _segment_sum(src, seg, n):
    return jax.ops.segment_sum(src, seg, n)
kernel_name = 'mk_recurrent_d2_jaxref_r4_d6d27f'

def setup_inputs(seed: int=0):
    np.random.seed(seed)
    _w = jnp.asarray

    def _L0_attn_setup():
        import jax, jax.numpy as jnp
        import numpy as np
        import math
        D_MODEL = 256
        N_HEAD = 16
        D_HEAD = D_MODEL // N_HEAD
        D_KMAP = 128
        D_INNER = 1024

        def _layer_norm(x, g, b, eps=1e-05):
            mu = jnp.mean(x, axis=-1, keepdims=True)
            var = jnp.mean(jnp.square(x - mu), axis=-1, keepdims=True)
            return (x - mu) * jax.lax.rsqrt(var + eps) * g + b

        def _fourier_kernel(x, proj_mat):
            p = jnp.einsum('blhd,dm->blhm', x, proj_mat) / math.sqrt(D_HEAD)
            return jnp.concatenate([jnp.cos(p), jnp.sin(p)], axis=-1) / math.sqrt(D_KMAP)
        key = jax.random.key(seed)
        ks = jax.random.split(key, 12)
        s = 0.02
        return {'x': jax.random.normal(ks[0], (4, 1024, D_MODEL), dtype=jnp.float32), 'proj_mat': jax.random.normal(ks[1], (D_HEAD, D_KMAP), dtype=jnp.float32), 'wq': jax.random.normal(ks[2], (D_MODEL, D_MODEL), dtype=jnp.float32) * s, 'bq': jnp.zeros((D_MODEL,), jnp.float32), 'wk': jax.random.normal(ks[3], (D_MODEL, D_MODEL), dtype=jnp.float32) * s, 'bk': jnp.zeros((D_MODEL,), jnp.float32), 'wv': jax.random.normal(ks[4], (D_MODEL, D_MODEL), dtype=jnp.float32) * s, 'bv': jnp.zeros((D_MODEL,), jnp.float32), 'wo': jax.random.normal(ks[5], (D_MODEL, D_MODEL), dtype=jnp.float32) * s, 'bo': jnp.zeros((D_MODEL,), jnp.float32), 'ln1_g': jnp.ones((D_MODEL,), jnp.float32), 'ln1_b': jnp.zeros((D_MODEL,), jnp.float32), 'w1': jax.random.normal(ks[6], (D_MODEL, D_INNER), dtype=jnp.float32) * s, 'b1': jnp.zeros((D_INNER,), jnp.float32), 'w2': jax.random.normal(ks[7], (D_INNER, D_MODEL), dtype=jnp.float32) * s, 'b2': jnp.zeros((D_MODEL,), jnp.float32), 'ln2_g': jnp.ones((D_MODEL,), jnp.float32), 'ln2_b': jnp.zeros((D_MODEL,), jnp.float32)}
    _L0_attn_in = _L0_attn_setup()

    def _L0_ffn_setup():
        import jax, jax.numpy as jnp
        import numpy as np
        DIM = 256

        def _reference_tuple_inner(x, W_r, W_k, W_v, mu_r, mu_k):
            B, T, C = x.shape
            x_prev = jnp.concatenate([jnp.zeros((B, 1, C), x.dtype), x[:, :-1, :]], axis=1)
            xr = mu_r * x + (1.0 - mu_r) * x_prev
            xk = mu_k * x + (1.0 - mu_k) * x_prev
            r = jax.nn.sigmoid(jnp.einsum('btc,dc->btd', xr, W_r))
            k = jnp.einsum('btc,dc->btd', xk, W_k)
            k_act = jnp.square(jax.nn.relu(k))
            out = r * jnp.einsum('btc,dc->btd', k_act, W_v)
            new_state = x[:, -1, :]
            return (out, new_state)
        key = jax.random.key(seed)
        ks = jax.random.split(key, 6)
        B, T, C = (8, 512, DIM)
        x = jax.random.normal(ks[0], (B, T, C), dtype=jnp.float32)
        s = 1.0 / np.sqrt(C)
        W_r = jax.random.uniform(ks[1], (C, C), jnp.float32, -s, s)
        W_k = jax.random.uniform(ks[2], (C, C), jnp.float32, -s, s)
        W_v = jax.random.uniform(ks[3], (C, C), jnp.float32, -s, s)
        mu_r = jax.random.uniform(ks[4], (C,), jnp.float32)
        mu_k = jax.random.uniform(ks[5], (C,), jnp.float32)
        return {'x': x, 'W_r': W_r, 'W_k': W_k, 'W_v': W_v, 'mu_r': mu_r, 'mu_k': mu_k}
    _L0_ffn_in = _L0_ffn_setup()

    def _L1_attn_setup():
        import jax, jax.numpy as jnp
        import numpy as np
        D_MODEL = 256
        D_STATE = 16
        D_CONV = 4
        EXPAND = 2
        D_INNER = EXPAND * D_MODEL
        DT_RANK = D_MODEL // 16
        BATCH = 4
        SEQ = 512
        key = jax.random.key(seed)
        ks = jax.random.split(key, 9)
        s = lambda k, shape, sc: jax.random.normal(k, shape, jnp.float32) * sc
        x = s(ks[0], (BATCH, SEQ, D_MODEL), 1.0)
        W_in = s(ks[1], (2 * D_INNER, D_MODEL), D_MODEL ** (-0.5))
        conv_w = s(ks[2], (D_INNER, D_CONV), D_CONV ** (-0.5))
        conv_b = s(ks[3], (D_INNER,), 0.02)
        W_xproj = s(ks[4], (DT_RANK + 2 * D_STATE, D_INNER), D_INNER ** (-0.5))
        W_dt = s(ks[5], (D_INNER, DT_RANK), DT_RANK ** (-0.5))
        b_dt = jax.random.uniform(ks[6], (D_INNER,), jnp.float32, -4.0, -1.0)
        A_log = jnp.log(jnp.tile(jnp.arange(1, D_STATE + 1, dtype=jnp.float32), (D_INNER, 1)))
        D_skip = jnp.ones((D_INNER,), jnp.float32)
        W_out = s(ks[7], (D_MODEL, D_INNER), D_INNER ** (-0.5))
        return dict(x=x, W_in=W_in, conv_w=conv_w, conv_b=conv_b, W_xproj=W_xproj, W_dt=W_dt, b_dt=b_dt, A_log=A_log, D_skip=D_skip, W_out=W_out)
    _L1_attn_in = _L1_attn_setup()

    def _L1_ffn_setup():
        import jax, jax.numpy as jnp
        import numpy as np
        D = 256
        E = 8
        H = 512
        TOP_K = 2
        ALPHA = 0.5
        LN_EPS = 1e-05

        def _experts_all(x, W1, b1, W2, b2):
            h = jax.nn.relu(jnp.einsum('bld,edh->eblh', x, W1) + b1[:, None, None, :])
            return jnp.einsum('eblh,ehd->ebld', h, W2) + b2[:, None, None, :]

        def _selected_expert(x, expert_idx, W1, b1, W2, b2):
            oh = jax.nn.one_hot(expert_idx, E, dtype=x.dtype)
            return jnp.einsum('ebld,ble->bld', _experts_all(x, W1, b1, W2, b2), oh)

        def _layer_norm(x, gamma, beta):
            mu = jnp.mean(x, axis=-1, keepdims=True)
            var = jnp.mean(jnp.square(x - mu), axis=-1, keepdims=True)
            return (x - mu) * jax.lax.rsqrt(var + LN_EPS) * gamma + beta
        key = jax.random.key(seed)
        ks = jax.random.split(key, 8)
        x = jax.random.normal(ks[0], (2, 512, D), dtype=jnp.float32)
        gate_W = jax.random.normal(ks[1], (D, E), dtype=jnp.float32) * 0.02
        gate_b = jnp.zeros((E,), dtype=jnp.float32)
        W1 = jax.random.normal(ks[2], (E, D, H), dtype=jnp.float32) * 0.02
        b1 = jnp.zeros((E, H), dtype=jnp.float32)
        W2 = jax.random.normal(ks[3], (E, H, D), dtype=jnp.float32) * 0.02
        b2 = jnp.zeros((E, D), dtype=jnp.float32)
        ln_gamma = jnp.ones((D,), dtype=jnp.float32)
        ln_beta = jnp.zeros((D,), dtype=jnp.float32)
        return {'x': x, 'gate_W': gate_W, 'gate_b': gate_b, 'W1': W1, 'b1': b1, 'W2': W2, 'b2': b2, 'ln_gamma': ln_gamma, 'ln_beta': ln_beta}
    _L1_ffn_in = _L1_ffn_setup()
    _d = {'L0_attn_x': _L0_attn_in['x'], 'L0_attn_proj_mat': _L0_attn_in['proj_mat'], 'L0_attn_wq': _L0_attn_in['wq'], 'L0_attn_bq': _L0_attn_in['bq'], 'L0_attn_wk': _L0_attn_in['wk'], 'L0_attn_bk': _L0_attn_in['bk'], 'L0_attn_wv': _L0_attn_in['wv'], 'L0_attn_bv': _L0_attn_in['bv'], 'L0_attn_wo': _L0_attn_in['wo'], 'L0_attn_bo': _L0_attn_in['bo'], 'L0_attn_ln1_g': _L0_attn_in['ln1_g'], 'L0_attn_ln1_b': _L0_attn_in['ln1_b'], 'L0_attn_w1': _L0_attn_in['w1'], 'L0_attn_b1': _L0_attn_in['b1'], 'L0_attn_w2': _L0_attn_in['w2'], 'L0_attn_b2': _L0_attn_in['b2'], 'L0_attn_ln2_g': _L0_attn_in['ln2_g'], 'L0_attn_ln2_b': _L0_attn_in['ln2_b'], 'L0_ffn_W_r': _L0_ffn_in['W_r'], 'L0_ffn_W_k': _L0_ffn_in['W_k'], 'L0_ffn_W_v': _L0_ffn_in['W_v'], 'L0_ffn_mu_r': _L0_ffn_in['mu_r'], 'L0_ffn_mu_k': _L0_ffn_in['mu_k'], 'L1_attn_W_in': _L1_attn_in['W_in'], 'L1_attn_conv_w': _L1_attn_in['conv_w'], 'L1_attn_conv_b': _L1_attn_in['conv_b'], 'L1_attn_W_xproj': _L1_attn_in['W_xproj'], 'L1_attn_W_dt': _L1_attn_in['W_dt'], 'L1_attn_b_dt': _L1_attn_in['b_dt'], 'L1_attn_A_log': _L1_attn_in['A_log'], 'L1_attn_D_skip': _L1_attn_in['D_skip'], 'L1_attn_W_out': _L1_attn_in['W_out'], 'L1_ffn_gate_W': _L1_ffn_in['gate_W'], 'L1_ffn_gate_b': _L1_ffn_in['gate_b'], 'L1_ffn_W1': _L1_ffn_in['W1'], 'L1_ffn_b1': _L1_ffn_in['b1'], 'L1_ffn_W2': _L1_ffn_in['W2'], 'L1_ffn_b2': _L1_ffn_in['b2'], 'L1_ffn_ln_gamma': _L1_ffn_in['ln_gamma'], 'L1_ffn_ln_beta': _L1_ffn_in['ln_beta']}
    _x0 = _d['L0_attn_x']
    _d['L0_attn_x'] = jax.random.normal(jax.random.fold_in(jax.random.key(seed), 1), (4, 1024, 256), dtype=_x0.dtype)
    del _x0
    return _d

def reference(L0_attn_x, L0_attn_proj_mat, L0_attn_wq, L0_attn_bq, L0_attn_wk, L0_attn_bk, L0_attn_wv, L0_attn_bv, L0_attn_wo, L0_attn_bo, L0_attn_ln1_g, L0_attn_ln1_b, L0_attn_w1, L0_attn_b1, L0_attn_w2, L0_attn_b2, L0_attn_ln2_g, L0_attn_ln2_b, L0_ffn_W_r, L0_ffn_W_k, L0_ffn_W_v, L0_ffn_mu_r, L0_ffn_mu_k, L1_attn_W_in, L1_attn_conv_w, L1_attn_conv_b, L1_attn_W_xproj, L1_attn_W_dt, L1_attn_b_dt, L1_attn_A_log, L1_attn_D_skip, L1_attn_W_out, L1_ffn_gate_W, L1_ffn_gate_b, L1_ffn_W1, L1_ffn_b1, L1_ffn_W2, L1_ffn_b2, L1_ffn_ln_gamma, L1_ffn_ln_beta):

    def _L0_attn_ref(x, proj_mat, wq, bq, wk, bk, wv, bv, wo, bo, ln1_g, ln1_b, w1, b1, w2, b2, ln2_g, ln2_b):
        import jax, jax.numpy as jnp
        import numpy as np
        import math
        D_MODEL = 256
        N_HEAD = 16
        D_HEAD = D_MODEL // N_HEAD
        D_KMAP = 128
        D_INNER = 1024

        def _layer_norm(x, g, b, eps=1e-05):
            mu = jnp.mean(x, axis=-1, keepdims=True)
            var = jnp.mean(jnp.square(x - mu), axis=-1, keepdims=True)
            return (x - mu) * jax.lax.rsqrt(var + eps) * g + b

        def _fourier_kernel(x, proj_mat):
            p = jnp.einsum('blhd,dm->blhm', x, proj_mat) / math.sqrt(D_HEAD)
            return jnp.concatenate([jnp.cos(p), jnp.sin(p)], axis=-1) / math.sqrt(D_KMAP)
        B, L, _ = x.shape
        x2 = _layer_norm(x, ln1_g, ln1_b)
        q = (x2 @ wq + bq).reshape(B, L, N_HEAD, D_HEAD)
        k = (x2 @ wk + bk).reshape(B, L, N_HEAD, D_HEAD)
        v = (x2 @ wv + bv).reshape(B, L, N_HEAD, D_HEAD)
        qp = _fourier_kernel(q, proj_mat)
        kp = _fourier_kernel(k, proj_mat)
        kv = jnp.einsum('blhm,blhd->bhmd', kp, v)
        attn = jnp.einsum('blhm,bhmd->blhd', qp, kv)
        attn = attn.reshape(B, L, D_MODEL) @ wo + bo
        x = x + attn
        x2 = _layer_norm(x, ln2_g, ln2_b)
        h = jax.nn.relu(x2 @ w1 + b1)
        x = x + (h @ w2 + b2)
        return x

    def _L0_ffn_ref(x, W_r, W_k, W_v, mu_r, mu_k):
        import jax, jax.numpy as jnp
        import numpy as np
        DIM = 256

        def _reference_tuple_inner(x, W_r, W_k, W_v, mu_r, mu_k):
            B, T, C = x.shape
            x_prev = jnp.concatenate([jnp.zeros((B, 1, C), x.dtype), x[:, :-1, :]], axis=1)
            xr = mu_r * x + (1.0 - mu_r) * x_prev
            xk = mu_k * x + (1.0 - mu_k) * x_prev
            r = jax.nn.sigmoid(jnp.einsum('btc,dc->btd', xr, W_r))
            k = jnp.einsum('btc,dc->btd', xk, W_k)
            k_act = jnp.square(jax.nn.relu(k))
            out = r * jnp.einsum('btc,dc->btd', k_act, W_v)
            new_state = x[:, -1, :]
            return (out, new_state)
        return _reference_tuple_inner(x, W_r, W_k, W_v, mu_r, mu_k)[0]

    def _L1_attn_ref(x, W_in, conv_w, conv_b, W_xproj, W_dt, b_dt, A_log, D_skip, W_out):
        import jax, jax.numpy as jnp
        import numpy as np
        D_MODEL = 256
        D_STATE = 16
        D_CONV = 4
        EXPAND = 2
        D_INNER = EXPAND * D_MODEL
        DT_RANK = D_MODEL // 16
        BATCH = 4
        SEQ = 512
        silu = jax.nn.silu
        xz = jnp.einsum('bld,ed->ble', x, W_in)
        xi, z = jnp.split(xz, 2, axis=-1)
        K = conv_w.shape[1]
        L = xi.shape[1]
        xpad = jnp.pad(xi, ((0, 0), (K - 1, 0), (0, 0)))
        xc = sum((xpad[:, k:k + L, :] * conv_w[:, k] for k in range(K)))
        u = silu(xc + conv_b)
        dbl = jnp.einsum('blc,ec->ble', u, W_xproj)
        dt = jax.nn.softplus(jnp.einsum('blr,cr->blc', dbl[..., :DT_RANK], W_dt) + b_dt)
        Bs = dbl[..., DT_RANK:DT_RANK + D_STATE]
        Cs = dbl[..., DT_RANK + D_STATE:]
        A = -jnp.exp(A_log)

        def step(h, inp):
            dt_t, B_t, C_t, u_t = inp
            dA = jnp.exp(dt_t[:, :, None] * A)
            h = h * dA + (dt_t * u_t)[:, :, None] * B_t[:, None, :]
            y = jnp.einsum('bcs,bs->bc', h, C_t)
            return (h, y)
        h0 = jnp.zeros((x.shape[0], D_INNER, D_STATE), x.dtype)
        xs = (jnp.swapaxes(dt, 0, 1), jnp.swapaxes(Bs, 0, 1), jnp.swapaxes(Cs, 0, 1), jnp.swapaxes(u, 0, 1))
        _, ys = jax.lax.scan(step, h0, xs)
        y = jnp.swapaxes(ys, 0, 1) + u * D_skip
        y = y * silu(z)
        return jnp.einsum('blc,dc->bld', y, W_out)

    def _L1_ffn_ref(x, gate_W, gate_b, W1, b1, W2, b2, ln_gamma, ln_beta):
        import jax, jax.numpy as jnp
        import numpy as np
        D = 256
        E = 8
        H = 512
        TOP_K = 2
        ALPHA = 0.5
        LN_EPS = 1e-05

        def _experts_all(x, W1, b1, W2, b2):
            h = jax.nn.relu(jnp.einsum('bld,edh->eblh', x, W1) + b1[:, None, None, :])
            return jnp.einsum('eblh,ehd->ebld', h, W2) + b2[:, None, None, :]

        def _selected_expert(x, expert_idx, W1, b1, W2, b2):
            oh = jax.nn.one_hot(expert_idx, E, dtype=x.dtype)
            return jnp.einsum('ebld,ble->bld', _experts_all(x, W1, b1, W2, b2), oh)

        def _layer_norm(x, gamma, beta):
            mu = jnp.mean(x, axis=-1, keepdims=True)
            var = jnp.mean(jnp.square(x - mu), axis=-1, keepdims=True)
            return (x - mu) * jax.lax.rsqrt(var + LN_EPS) * gamma + beta
        residual = x
        gate_logits = jnp.einsum('bld,de->ble', x, gate_W) + gate_b
        gate_weights = jax.nn.softmax(gate_logits, axis=-1)
        topk_vals, topk_idx = jax.lax.top_k(gate_weights, TOP_K)
        boost = jax.lax.stop_gradient(x)
        outs = []
        for i in range(TOP_K):
            eo = _selected_expert(boost, topk_idx[:, :, i], W1, b1, W2, b2)
            outs.append(eo)
            if i < TOP_K - 1:
                boost = boost + ALPHA * jax.lax.stop_gradient(eo)
        fused = sum((topk_vals[:, :, i:i + 1] * outs[i] for i in range(TOP_K)))
        return _layer_norm(residual + fused, ln_gamma, ln_beta)
    x = L0_attn_x
    xn = _layernorm(x, axis=-1)
    s = _L0_attn_ref(xn, L0_attn_proj_mat, L0_attn_wq, L0_attn_bq, L0_attn_wk, L0_attn_bk, L0_attn_wv, L0_attn_bv, L0_attn_wo, L0_attn_bo, L0_attn_ln1_g, L0_attn_ln1_b, L0_attn_w1, L0_attn_b1, L0_attn_w2, L0_attn_b2, L0_attn_ln2_g, L0_attn_ln2_b)
    g = _silu(_L0_ffn_ref(xn, L0_ffn_W_r, L0_ffn_W_k, L0_ffn_W_v, L0_ffn_mu_r, L0_ffn_mu_k))
    x = x + s * g
    xn = _layernorm(x, axis=-1)
    s = _L1_attn_ref(xn, L1_attn_W_in, L1_attn_conv_w, L1_attn_conv_b, L1_attn_W_xproj, L1_attn_W_dt, L1_attn_b_dt, L1_attn_A_log, L1_attn_D_skip, L1_attn_W_out)
    g = _silu(_L1_ffn_ref(xn, L1_ffn_gate_W, L1_ffn_gate_b, L1_ffn_W1, L1_ffn_b1, L1_ffn_W2, L1_ffn_b2, L1_ffn_ln_gamma, L1_ffn_ln_beta))
    x = x + s * g
    return x

_drawn_inputs = setup_inputs


def setup_inputs(seed=0):
    import zlib

    import numpy as np

    out = dict(_drawn_inputs(seed))
    spreads = {'L0_attn_bq': (0.0, 0.8),
     'L0_attn_bk': (0.0, 0.8),
     'L0_attn_bv': (0.0, 0.1),
     'L0_attn_bo': (0.0, 0.8),
     'L0_attn_ln1_g': (1.0, 0.6),
     'L0_attn_ln1_b': (0.0, 0.1),
     'L0_attn_b1': (0.0, 0.8),
     'L0_attn_b2': (0.0, 0.8),
     'L0_attn_ln2_g': (1.0, 0.6),
     'L0_attn_ln2_b': (0.0, 0.8),
     'L1_attn_D_skip': (1.0, 0.2),
     'L1_ffn_gate_b': (0.0, 0.8),
     'L1_ffn_b1': (0.0, 0.8),
     'L1_ffn_b2': (0.0, 2.0),
     'L1_ffn_ln_gamma': (1.0, 0.2),
     'L1_ffn_ln_beta': (0.0, 0.543)}
    factors = {'L0_attn_proj_mat': 8.0,
     'L0_attn_wq': 2.869,
     'L0_attn_wk': 8.0,
     'L0_attn_w1': 8.0,
     'L0_attn_w2': 8.0,
     'L1_attn_conv_b': 8.0,
     'L1_ffn_gate_W': 8.0,
     'L1_ffn_W1': 8.0,
     'L1_ffn_W2': 8.0}
    for name, (base, spread) in spreads.items():
        noise = np.random.default_rng([zlib.crc32(name.encode()), seed]).standard_normal(out[name].shape)
        drawn = base * np.exp(spread * noise) if base else spread * noise
        out[name] = jnp.asarray(drawn.astype(out[name].dtype))
    for name, factor in factors.items():
        out[name] = (out[name] * factor).astype(out[name].dtype)
    return out
```

```python
import numpy as np
from contextlib import ExitStack
import concourse.bass as bass
from concourse import mybir

F32 = mybir.dt.float32
BF16 = mybir.dt.bfloat16
I32 = mybir.dt.int32
ALU = mybir.AluOpType
ACT = mybir.ActivationFunctionType
AX = mybir.AxisListType

B, L, D = 4, 1024, 256
P = 128
TB = L // P
NT = B * TB
KD = D // P
CH = 512
NC_ = L // CH
EPS = 1e-5

H, DH, M = 16, 16, 128
FF = 1024
MF = FF // P
ROUND = 1.5 * 2.0 ** 23
TURN = float(np.nextafter(np.float32(2 * np.pi), np.float32(0)))
RSQRT_SEED = float(0x5F3759DF)

E, HE = 8, 512


class Ring:

    def __init__(self, names, n):
        self.n = n
        self.of = {}
        self.uses = [0] * n
        for i, name in enumerate(names):
            s = i % n
            self.of[name] = (s, self.uses[s])
            self.uses[s] += 1


JOBS_A = (
    [("xt", c) for c in range(NC_)] + [("x2", c) for c in range(NC_)]
    + [("q", m) for m in range(KD)] + [("k", m) for m in range(KD)] + [("v", i) for i in range(2)]
    + [("kf", n) for n in range(16)] + [("qf", n) for n in range(16)]
    + [("wo", i) for i in range(2)] + [("xf", c) for c in range(NC_)]
    + [j for c in range(NC_) for j in [("h", c, q) for q in range(MF // 2)] + [("w2", c)]]
    + [("r", i) for i in range(2)] + [("kk", m) for m in range(KD)] + [("vv", i) for i in range(2)]
    + [("xn", c) for c in range(NC_)] + [("gate",)]
)


def phase_a(nc, g):
    ring = Ring(JOBS_A, 3)
    ctx = ExitStack()
    with ctx:
        def sb(name, shape, dt=F32):
            return ctx.enter_context(nc.sbuf_tensor(name, shape, dt))

        def sem(name):
            return ctx.enter_context(nc.semaphore(name))

        wq, wk, wv, wo = (sb(n, [P, KD, D]) for n in ("wq", "wk", "wv", "wo"))
        wr, wkk, wvv = (sb(n, [P, KD, D]) for n in ("wr", "wkk", "wvv"))
        w1 = sb("w1", [P, KD, FF])
        w2 = sb("w2", [P, MF, D])
        gate_w = sb("gate_w", [P, KD, E])
        proj = sb("proj", [P, 2, M])
        cols = sb("cols", [P, 8, KD])
        b1c = sb("b1c", [P, MF])
        omu = sb("omu", [P, 2, KD])
        ident = sb("ident_a", [P, P])
        halfpi = sb("halfpi", [P, 1])
        rnd = sb("rnd", [P, 1])
        brow = sb("brow", [1, 3 * D + E])
        bsp = sb("bsp", [1, 3, 3 * D + E], BF16)
        brs = sb("brs", [1, 3 * D + E])
        bias3 = sb("bias3", [3, 3 * D + E], BF16)
        ones3 = sb("ones3", [3, P], BF16)

        xin = sb("xin", [P, TB, D])
        xres = sb("xres", [P, TB, D])
        xn = sb("xn_a", [P, TB, D])
        xh = sb("xh", [P, TB, D])
        s1 = sb("s1", [P, TB, D])
        st = sb("st_a", [P, TB, 6])
        mv = sb("mv_a", [P, TB, 2])
        rs = sb("rs_a", [P, 4, TB])
        spare = sb("spare_a", [P, 1])
        xnT = sb("xnT_a", [P, KD, 1 + L])
        x2T = sb("x2T", [P, KD, L])
        qkh = sb("qkh", [P, MF, CH])
        qT = qkh[:, 0:4, :].rearrange("p (m c) t -> p m (c t)", m=KD)
        kT = qkh[:, 4:8, :].rearrange("p (m c) t -> p m (c t)", m=KD)
        v = sb("v", [P, TB, D])
        turns = sb("turns", [P, 2 * CH])
        rr = sb("rr", [P, 2, 2 * CH])
        ra = sb("ra", [P, 2, 2 * CH])
        fs = sb("fs", [P, 2, 2 * CH])
        fc = sb("fc", [P, 2, 2 * CH])
        kv = sb("kv", [P, H // 2, 2, 2, 2 * DH])
        aT = sb("aT", [P, KD, L])
        xr = sb("xr", [P, KD, L])
        xk = sb("xk", [P, KD, L])
        kr = sb("kr", [P, KD, L])

        W = [ctx.enter_context(nc.psum_tensor(f"work{i}", [P, 2 * CH], F32)) for i in range(3)]
        kvp = ctx.enter_context(nc.psum_tensor("kvp", [P, H * 2 * DH], F32))
        atp = ctx.enter_context(nc.psum_tensor("atp", [P, CH], F32))

        w_in = sem("w_in"); bias_in = sem("bias_in"); bias_split = sem("bias_split")
        zeroed = sem("zeroed"); prep = sem("prep")
        xin_in = sem("xin_in"); xres_in = sem("xres_in"); stored = sem("stored")
        full = [sem(f"full{i}") for i in range(3)]
        dve = sem("dve_chain")
        xn_ok = sem("xn_ok"); xh_ok = sem("xh_ok"); s1_ok = sem("s1_ok")
        tr_ok = sem("tr_ok"); qk_ok = sem("qk_ok"); v_ok = sem("v_ok")
        turns_ok = sem("turns_ok"); rr_ok = sem("rr_ok"); ra_ok = sem("ra_ok")
        feat_ok = sem("feat_ok"); feat_used = sem("feat_used")
        kv_ok = sem("kv_ok"); at_ok = sem("at_ok")
        h_ok = sem("h_ok"); mix_ok = sem("mix_ok"); th_ok = sem("th_ok")
        kr_ok = sem("kr_ok"); kact_ok = sem("kact_ok"); out_ok = sem("out_ok"); g_ok = sem("g_ok")
        x1_ok = sem("x1_ok"); xnT_ok = sem("xnT_ok"); lg_ok = sem("lg_ok")

        READ = {}
        for c in range(NC_):
            READ["xt", c] = (tr_ok, 6, c + 1)
            READ["x2", c] = (tr_ok, 6, c + 3)
            READ["xf", c] = (tr_ok, 6, c + 5)
            READ["w2", c] = (s1_ok, 4, c + 3)
            READ["xn", c] = (xnT_ok, 2, c + 1)
            for q in range(MF // 2):
                READ["h", c, q] = (h_ok, MF, c * MF // 2 + q + 1)
        for m in range(KD):
            READ["q", m] = (qk_ok, 4, m + 1)
            READ["k", m] = (qk_ok, 4, m + 3)
            READ["kk", m] = (kr_ok, 2, m + 1)
        for i in range(2):
            READ["v", i] = (v_ok, 2, i + 1)
            READ["wo", i] = (s1_ok, 4, i + 1)
            READ["r", i] = (th_ok, 2, i + 1)
            READ["vv", i] = (out_ok, 2, i + 1)
        for n in range(16):
            READ["kf", n] = (rr_ok, 32, n + 1)
            READ["qf", n] = (rr_ok, 32, n + 17)
        READ["gate",] = (lg_ok, 1, 1)

        def slot(*job):
            return W[ring.of[job][0]]

        def wait_full(e, b, *job):
            s, use = ring.of[job]
            e.wait_ge(full[s], b * ring.uses[s] + use + 1)

        def wait_slot(e, b, *job):
            at = JOBS_A.index(job)
            if at >= 3:
                s, per, k = READ[JOBS_A[at - 3]]
                e.wait_ge(s, b * per + k)

        with nc.Block() as block:
            @block.sync
            def _(sp):
                def load(dst, src):
                    sp.dma_start(dst, src).then_inc(w_in, 16)

                tokens = lambda ap: ap.rearrange("(t p) d -> p t d", p=P)
                sp.dma_start(xin[:, :, :], tokens(g["x"][0])).then_inc(xin_in, 16)
                load(ident[:, :], g["ident"])
                with nc.allow_non_contiguous_dma(reason="vectors by channel, once"):
                    for i, n in enumerate(("bq", "bk", "ln1_g", "ln1_b", "ln2_g", "ln2_b", "mu_r", "mu_k")):
                        load(cols[:, i, :], g[n].rearrange("(k p) -> p k", p=P))
                    load(b1c[:, :], g["b1"].rearrange("(k p) -> p k", p=P))
                for i, n in enumerate(("bv", "bo", "b2", "gate_b")):
                    load(brow[:, i * D:i * D + g[n].shape[0]], g[n].rearrange("(a n) -> a n", a=1))
                for t, n in ((wq, "wq"), (wk, "wk"), (wv, "wv"), (wo, "wo"), (wr, "W_rT"), (wkk, "W_kT"), (wvv, "W_vT"),
                             (w1, "w1"), (w2, "w2"), (gate_w, "gate_W")):
                    load(t[:, :, :], g[n].rearrange("(k p) n -> p k n", p=P))
                sp.wait_ge(zeroed, 1)
                for r in range(4):
                    for e in range(2):
                        load(proj[32 * r + 16 * e:32 * r + 16 * e + 16, e, :], g["proj"])
                sp.wait_ge(bias_split, 6)
                for i in range(3):
                    sp.dma_start(bias3[i:i + 1, :], bsp[:, i, :]).then_inc(bias_in, 16)

                def batch(b, last):
                    sp.dma_start(xres[:, :, :], tokens(g["x"][b])).then_inc(xres_in, 16)
                    if not last:
                        sp.wait_ge(xn_ok, b * TB + TB)
                        sp.dma_start(xin[:, :, :], tokens(g["x"][b + 1])).then_inc(xin_in, 16)
                    sp.wait_ge(x1_ok, b + 1)
                    sp.dma_start(tokens(g["x1_s"][b]), s1[:, :, :]).then_inc(stored, 16)
                    sp.wait_ge(xh_ok, b * 3 * TB + 3 * TB)
                    sp.dma_start(tokens(g["xn1_s"][b]), xh[:, :, :]).then_inc(stored, 16)
                    sp.wait_ge(xnT_ok, b * NC_ + NC_)
                    sp.dma_start(g["xn1T_s"][b], kr[:, :, :]).then_inc(stored, 16)

                with sp.Fori(0, B - 1) as b:
                    batch(b, False)
                batch(B - 1, True)
                sp.wait_ge(stored, 48 * B)

            @block.gpsimd
            def _(pool):
                nc.gpsimd.memset(proj[:, :, :], 0.0).then_inc(zeroed, 1)
                nc.gpsimd.memset(halfpi[:, :], float(np.float32(np.pi / 2))).then_inc(prep, 1)
                nc.gpsimd.memset(rnd[:, :], ROUND).then_inc(prep, 1)
                nc.gpsimd.memset(ones3[:, :], 1.0).then_inc(prep, 1)
                nc.gpsimd.memset(kv[:, :, :, :, :], 0.0).then_inc(prep, 1)
                nc.gpsimd.memset(xnT[:, :, 0:1], 0.0).then_inc(prep, 1)
                with pool.Fori(0, B) as b:
                    for m in range(KD):
                        pool.wait_ge(kr_ok, b * KD + m + 1)
                        nc.gpsimd.tensor_tensor(aT[:, m, :], kr[:, m, :], kr[:, m, :], ALU.mult).then_inc(kact_ok, 1)

            LN_LINKS = 2 * TB + 1 + 3 + 16
            DVE_LINKS = 4 * LN_LINKS + 2 * KD + 2

            def layer_norm_stats(v_, link, src, ready=None):
                for t in range(TB):
                    if ready:
                        ready(t)
                    v_.bn_stats(st[:, t, :], src[:, t, :]).then_inc(dve, 1)
                link(TB)
                v_.memset(spare[:, :], 0.0).then_inc(dve, 1)
                for t in range(TB):
                    v_.bn_aggr(mv[:, t, :], st[:, t, :]).then_inc(dve, 1)
                link(TB + 1)
                var, y, y2, h = (rs[:, i, :] for i in range(4))
                v_.tensor_scalar(var, mv[:, :, 1], EPS, None, ALU.add).then_inc(dve, 1)
                link(1)
                v_.tensor_scalar(h.bitcast(I32), var.bitcast(I32), 1, None, ALU.logical_shift_right).then_inc(dve, 1)
                link(1)
                v_.tensor_scalar(y.bitcast(I32), h.bitcast(I32), -1.0, RSQRT_SEED, ALU.mult, ALU.add).then_inc(dve, 1)
                link(1)
                for _ in range(4):
                    v_.tensor_tensor(y2, y, y, ALU.mult).then_inc(dve, 1)
                    link(1)
                    v_.tensor_tensor(y2, y2, var, ALU.mult).then_inc(dve, 1)
                    link(1)
                    v_.tensor_scalar(y2, y2, -0.5, 1.5, ALU.mult, ALU.add).then_inc(dve, 1)
                    link(1)
                    v_.tensor_tensor(y, y, y2, ALU.mult).then_inc(dve, 1)
                    link(1)

            def normalise(v_, dst, src, ok):
                for t in range(TB):
                    v_.tensor_scalar(dst[:, t, :], src[:, t, :], mv[:, t, 0:1], rs[:, 1, t:t + 1],
                                     ALU.subtract, ALU.mult).then_inc(ok, 1)

            @block.vector
            def _(dv):
                v_ = nc.vector
                dv.wait_ge(w_in, 16 * (1 + 9 + 4 + 10 + 8))
                src = brow
                for i in range(3):
                    v_.tensor_copy(bsp[:, i, :], src[:, :]).then_inc(bias_split, 1)
                    dv.wait_ge(bias_split, 2 * i + 1)
                    v_.tensor_tensor(brs[:, :], src[:, :], bsp[:, i, :], ALU.subtract).then_inc(bias_split, 1)
                    dv.wait_ge(bias_split, 2 * i + 2)
                    src = brs
                v_.tensor_scalar(omu[:, :, :], cols[:, 6:8, :], -1.0, 1.0, ALU.mult, ALU.add).then_inc(prep, 1)
                v_.tensor_scalar(proj[:, :, :], proj[:, :, :], float(np.float32(1 / (8 * np.pi))), None, ALU.mult).then_inc(prep, 1)
                dv.wait_ge(prep, 7)

                def evac_attention(b, q):
                    dv.wait_ge(feat_used, b * 32 + 16 + 4 * q + 4)
                    v_.tensor_copy(aT[:, q // 2, (q % 2) * CH:(q % 2 + 1) * CH], atp[:, :]).then_inc(at_ok, 1)

                four = lambda ap, i: ap[:, 4 * i:4 * i + 4, :].rearrange("p t d -> p (t d)")
                with dv.Fori(0, B) as b:
                    n = [0]

                    def link(k):
                        n[0] += k
                        dv.wait_ge(dve, b * DVE_LINKS + n[0])

                    dv.wait_ge(xin_in, b * 16 + 16)
                    layer_norm_stats(v_, link, xin)
                    normalise(v_, xn, xin, xn_ok)
                    layer_norm_stats(v_, link, xn, lambda t: dv.wait_ge(xn_ok, b * TB + t + 1))
                    normalise(v_, xh, xn, xh_ok)
                    dv.wait_ge(tr_ok, b * 6 + 2)
                    for i, dst in enumerate((xr, xk)):
                        for k in range(KD):
                            v_.tensor_scalar(dst[:, k, :], xnT[:, k, 0:L], omu[:, i, k:k + 1], None, ALU.mult).then_inc(dve, 1)
                    link(2 * KD)
                    for i, dst in enumerate((xr, xk)):
                        for k in range(KD):
                            v_.scalar_tensor_tensor(dst[:, k, :], xnT[:, k, 1:L + 1], cols[:, 6 + i, k:k + 1], dst[:, k, :],
                                                    ALU.mult, ALU.add).then_inc(mix_ok, 1)
                    for i in range(2):
                        wait_full(dv, b, "v", i)
                        v_.tensor_copy(four(v, i), slot("v", i)[:, :]).then_inc(v_ok, 1)
                    for s in range(32):
                        job = ("kf", s) if s < 16 else ("qf", s - 16)
                        if s == 18:
                            dv.wait_ge(feat_used, b * 32 + 16)
                            sums = kvp[:, :].rearrange("p (a e c d) -> p a e c d", a=H // 2, e=2, c=2)
                            for e in range(2):
                                for cs in range(2):
                                    v_.tensor_scalar(kv[:, :, e, cs, DH * e:DH * e + DH], sums[:, :, e, cs, :], 1.0 / M, None,
                                                     ALU.mult).then_inc(kv_ok, 1)
                        dv.wait_ge(turns_ok, b * 32 + s + 1)
                        if s >= 2:
                            dv.wait_ge(feat_ok, b * 64 + 2 * (s - 1))
                        v_.scalar_tensor_tensor(rr[:, s % 2, :], turns[:, :], ROUND, slot(*job)[:, :],
                                                ALU.subtract, ALU.subtract).then_inc(rr_ok, 1)
                        dv.wait_ge(rr_ok, b * 32 + s + 1)
                        v_.tensor_scalar(ra[:, s % 2, :].bitcast(I32), rr[:, s % 2, :].bitcast(I32), 0x7FFFFFFF, None, ALU.bitwise_and).then_inc(ra_ok, 1)
                        if s >= 21 and s % 4 == 1:
                            evac_attention(b, (s - 21) // 4)
                    evac_attention(b, 3)
                    for i in range(2):
                        wait_full(dv, b, "wo", i)
                        v_.tensor_tensor(four(s1, i), slot("wo", i)[:, :], four(xn, i), ALU.add).then_inc(s1_ok, 1)
                    dv.wait_ge(s1_ok, b * 4 + 2)
                    layer_norm_stats(v_, link, s1)
                    normalise(v_, xh, s1, xh_ok)
                    for c in range(NC_):
                        wait_full(dv, b, "w2", c)
                        v_.tensor_tensor(four(s1, c), slot("w2", c)[:, :], four(s1, c), ALU.add).then_inc(s1_ok, 1)
                    for i in range(2):
                        wait_full(dv, b, "vv", i)
                        dv.wait_ge(th_ok, b * 2 + i + 1)
                        v_.scalar_tensor_tensor(four(v, i), four(v, i), 1.0, slot("vv", i)[:, :], ALU.add, ALU.mult).then_inc(out_ok, 1)
                    dv.wait_ge(s1_ok, b * 4 + 4)
                    for i in range(2):
                        dv.wait_ge(g_ok, b * 2 + i + 1)
                        v_.tensor_tensor(four(s1, i), four(s1, i), four(v, i), ALU.mult).then_inc(dve, 1)
                    link(2)
                    dv.wait_ge(xres_in, b * 16 + 16)
                    v_.tensor_tensor(s1[:, :, :], s1[:, :, :], xres[:, :, :], ALU.add).then_inc(x1_ok, 1)
                    dv.wait_ge(x1_ok, b + 1)
                    layer_norm_stats(v_, link, s1)
                    normalise(v_, xh, s1, xh_ok)
                    wait_full(dv, b, "gate")
                    v_.tensor_copy(g["lg"][:, bass.ds(b * TB, TB), :],
                                   slot("gate")[:, 0:TB * E].rearrange("p (t e) -> p t e", t=TB)).then_inc(lg_ok, 1)
                    dv.wait_ge(stored, b * 48 + 48)
                    assert n[0] == DVE_LINKS, (n[0], DVE_LINKS)

            @block.scalar
            def _(ac):
                A = nc.scalar.activation

                def copy_transposed(b, name, c, dst, ok, **scale):
                    wait_full(ac, b, name, c)
                    for k in range(KD):
                        i = A(dst(k), slot(name, c)[:, k * CH:(k + 1) * CH], ACT.Identity, **{n: f(k) for n, f in scale.items()})
                    i.then_inc(ok, 1)

                ac.wait_ge(w_in, 16 * (1 + 9 + 4 + 10 + 8))
                ac.wait_ge(prep, 7)
                with ac.Fori(0, B) as b:
                    for c in range(NC_):
                        copy_transposed(b, "xt", c, lambda k: xnT[:, k, 1 + c * CH:1 + (c + 1) * CH], tr_ok)
                    for c in range(NC_):
                        copy_transposed(b, "x2", c, lambda k: x2T[:, k, c * CH:(c + 1) * CH], tr_ok,
                                        scale=lambda k: cols[:, 2, k:k + 1], bias=lambda k: cols[:, 3, k:k + 1])
                    for i, (name, dst) in enumerate((("q", qT), ("k", kT))):
                        for m in range(KD):
                            wait_full(ac, b, name, m)
                            A(dst[:, m, :], slot(name, m)[:, :], ACT.Identity, bias=cols[:, i, m:m + 1]).then_inc(qk_ok, 1)

                    def whole_turns(s):
                        job = ("kf", s) if s < 16 else ("qf", s - 16)
                        wait_full(ac, b, *job)
                        if s:
                            ac.wait_ge(rr_ok, b * 32 + s)
                        A(turns[:, :], slot(*job)[:, :], ACT.Identity, bias=rnd[:, :]).then_inc(turns_ok, 1)

                    whole_turns(0)
                    for s in range(32):
                        if s < 31:
                            whole_turns(s + 1)
                        ac.wait_ge(rr_ok, b * 32 + s + 1)
                        if s >= 2:
                            ac.wait_ge(feat_used, b * 32 + s - 1)
                        A(fs[:, s % 2, :], rr[:, s % 2, :], ACT.Sin, scale=-TURN).then_inc(feat_ok, 1)
                        ac.wait_ge(ra_ok, b * 32 + s + 1)
                        A(fc[:, s % 2, :], ra[:, s % 2, :], ACT.Sin, scale=-TURN, bias=halfpi[:, :]).then_inc(feat_ok, 1)
                    for c in range(NC_):
                        copy_transposed(b, "xf", c, lambda k: x2T[:, k, c * CH:(c + 1) * CH], tr_ok,
                                        scale=lambda k: cols[:, 4, k:k + 1], bias=lambda k: cols[:, 5, k:k + 1])
                    for c in range(NC_):
                        for q in range(MF // 2):
                            wait_full(ac, b, "h", c, q)
                            if c and not q:
                                wait_full(ac, b, "w2", c - 1)
                            for j in range(2):
                                i = A(qkh[:, 2 * q + j, :], slot("h", c, q)[:, j * CH:(j + 1) * CH], ACT.Relu,
                                      bias=b1c[:, 2 * q + j:2 * q + j + 1])
                            i.then_inc(h_ok, 1)
                    for i in range(2):
                        wait_full(ac, b, "r", i)
                        A(v[:, 4 * i:4 * i + 4, :].rearrange("p t d -> p (t d)"), slot("r", i)[:, :], ACT.Tanh, scale=0.5).then_inc(th_ok, 1)
                    for m in range(KD):
                        wait_full(ac, b, "kk", m)
                        A(kr[:, m, :], slot("kk", m)[:, :], ACT.Relu).then_inc(kr_ok, 1)
                    for i in range(2):
                        ac.wait_ge(out_ok, b * 2 + i + 1)
                        A(v[:, 4 * i:4 * i + 4, :], v[:, 4 * i:4 * i + 4, :], ACT.Silu, scale=0.5).then_inc(g_ok, 1)
                    for c in range(NC_):
                        copy_transposed(b, "xn", c, lambda k: kr[:, k, c * CH:(c + 1) * CH], xnT_ok)

            @block.tensor
            def _(pe):
                mm = nc.tensor.matmul
                pe.wait_ge(w_in, 16 * (1 + 9 + 4 + 10 + 8))
                pe.wait_ge(prep, 7)
                pe.wait_ge(bias_in, 48)

                def done(ins, *job):
                    ins.then_inc(full[ring.of[job][0]], 1)

                def transposes(b, name, c, src):
                    wait_slot(pe, b, name, c)
                    for k in range(KD):
                        for t in range(4):
                            i = nc.tensor.transpose(slot(name, c)[:, k * CH + t * P:k * CH + (t + 1) * P],
                                                    src[:, 4 * c + t, k * P:(k + 1) * P], ident[:, :])
                    done(i, name, c)

                def by_channel(b, job, w, x, m):
                    wait_slot(pe, b, *job)
                    for c in range(NC_):
                        for k in range(KD):
                            i = mm(slot(*job)[:, c * CH:(c + 1) * CH], w[:, k, m * P:(m + 1) * P], x[:, k, c * CH:(c + 1) * CH],
                                   start=(k == 0), stop=(k == KD - 1))
                    done(i, *job)

                def by_token(b, job, x, w, bias, nk=KD):
                    wait_slot(pe, b, *job)
                    for t in range(4):
                        out = slot(*job)[:, t * D:(t + 1) * D]
                        for k in range(nk):
                            i = mm(out, x(k, t), w[:, k, :], start=(k == 0), stop=(k == nk - 1 and bias is None))
                        if bias is not None:
                            i = mm(out, ones3[:, :], bias3[:, bias * D:(bias + 1) * D], start=False, stop=True)
                    done(i, *job)

                with pe.Fori(0, B) as b:
                    for c in range(NC_):
                        pe.wait_ge(xn_ok, b * TB + 4 * c + 4)
                        transposes(b, "xt", c, xn)
                    for c in range(NC_):
                        pe.wait_ge(xh_ok, b * 3 * TB + 4 * c + 4)
                        transposes(b, "x2", c, xh)
                    pe.wait_ge(tr_ok, b * 6 + 4)
                    for m in range(KD):
                        by_channel(b, ("q", m), wq, x2T, m)
                    for m in range(KD):
                        by_channel(b, ("k", m), wk, x2T, m)
                    for i in range(2):
                        by_token(b, ("v", i), lambda k, t: x2T[:, k, (4 * i + t) * P:(4 * i + t + 1) * P], wv, 0)

                    def key_turns(s):
                        mt, j, tp = s // 8, s // 4 % 2, s % 4
                        wait_slot(pe, b, "kf", s)
                        if s == 0:
                            pe.wait_ge(qk_ok, b * 4 + 4)
                        for tt in range(2):
                            for i in range(2):
                                r = 32 * (2 * j + i)
                                t = 2 * tp + tt
                                ins = mm(slot("kf", s)[:, i * CH + tt * 2 * M:i * CH + (tt + 1) * 2 * M],
                                         kT[r:r + 32, mt, t * P:(t + 1) * P], proj[r:r + 32, :, :].rearrange("p e m -> p (e m)"),
                                         start=True, stop=True)
                        done(ins, "kf", s)

                    def query_turns(s):
                        mt, c, j, e = s // 8, s // 4 % 2, s // 2 % 2, s % 2
                        wait_slot(pe, b, "qf", s)
                        for i in range(2):
                            r = 32 * (2 * j + i)
                            ins = mm(slot("qf", s)[:, i * CH:(i + 1) * CH], proj[r:r + 32, e, :], qT[r:r + 32, mt, c * CH:(c + 1) * CH],
                                     start=True, stop=True)
                        done(ins, "qf", s)

                    def key_sums(s):
                        mt, j, tp = s // 8, s // 4 % 2, s % 4
                        pe.wait_ge(feat_ok, b * 64 + 2 * s + 2)
                        if s == 0:
                            pe.wait_ge(v_ok, b * 2 + 2)
                        for i in range(2):
                            for tt in range(2):
                                for e in range(2):
                                    head = (mt * 4 + 2 * j + i) * 2 + e
                                    at = ((i * 2 + tt) * 2 + e) * M
                                    for cs, f in enumerate((fs, fc)):
                                        first = s == 0 and i == tt == e == cs == 0
                                        last = s == 15 and i == tt == e == cs == 1
                                        ins = mm(kvp[:, (head * 2 + cs) * DH:(head * 2 + cs + 1) * DH], f[:, s % 2, at:at + M],
                                                 v[:, 2 * tp + tt, head * DH:(head + 1) * DH], start=first, stop=last,
                                                 skip_group_check=True)
                        ins.then_inc(feat_used, 1)

                    def attend(s):
                        mt, c, j, e = s // 8, s // 4 % 2, s // 2 % 2, s % 2
                        q = s // 4
                        pe.wait_ge(feat_ok, b * 64 + 32 + 2 * s + 2)
                        if s == 0:
                            pe.wait_ge(kv_ok, b * 4 + 4)
                        if s % 4 == 0 and q:
                            pe.wait_ge(at_ok, b * 4 + q)
                        for cs, f in enumerate((fs, fc)):
                            for i in range(2):
                                a = 2 * j + i
                                ins = mm(atp[32 * a:32 * a + 32, :], kv[:, mt * 4 + a, e, cs, :], f[:, s % 2, i * CH:(i + 1) * CH],
                                         start=(e == 0 and cs == 0), stop=(e == 1 and cs == 1))
                        return ins

                    for s in range(32 + 2):
                        if s < 32:
                            key_turns(s) if s < 16 else query_turns(s - 16)
                        u = s - 2
                        if 0 <= u < 16:
                            key_sums(u)
                        elif u >= 16:
                            attend(u - 16).then_inc(feat_used, 1)
                    pe.wait_ge(at_ok, b * 4 + 4)
                    for i in range(2):
                        by_token(b, ("wo", i), lambda k, t: aT[:, k, (4 * i + t) * P:(4 * i + t + 1) * P], wo, 1)
                    for c in range(NC_):
                        pe.wait_ge(xh_ok, b * 3 * TB + TB + 4 * c + 4)
                        transposes(b, "xf", c, xh)
                    for c in range(NC_):
                        pe.wait_ge(tr_ok, b * 6 + 5 + c)
                        for q in range(MF // 2):
                            wait_slot(pe, b, "h", c, q)
                            for j in range(2):
                                m = 2 * q + j
                                for k in range(KD):
                                    ins = mm(slot("h", c, q)[:, j * CH:(j + 1) * CH], w1[:, k, m * P:(m + 1) * P],
                                             x2T[:, k, c * CH:(c + 1) * CH], start=(k == 0), stop=(k == KD - 1))
                            done(ins, "h", c, q)
                        pe.wait_ge(h_ok, b * MF + (c + 1) * MF // 2)
                        by_token(b, ("w2", c), lambda k, t: qkh[:, k, t * P:(t + 1) * P], w2, 2, MF)
                    pe.wait_ge(mix_ok, b * 4 + 4)
                    for i in range(2):
                        by_token(b, ("r", i), lambda k, t: xr[:, k, (4 * i + t) * P:(4 * i + t + 1) * P], wr, None)
                    for m in range(KD):
                        by_channel(b, ("kk", m), wkk, xk, m)
                    pe.wait_ge(kact_ok, b * KD + KD)
                    for i in range(2):
                        by_token(b, ("vv", i), lambda k, t: aT[:, k, (4 * i + t) * P:(4 * i + t + 1) * P], wvv, None)
                    for c in range(NC_):
                        pe.wait_ge(xh_ok, b * 3 * TB + 2 * TB + 4 * c + 4)
                        transposes(b, "xn", c, xh)
                    wait_slot(pe, b, "gate")
                    pe.wait_ge(xnT_ok, b * 2 + 2)
                    for t in range(TB):
                        out = slot("gate")[:, t * E:(t + 1) * E]
                        for k in range(KD):
                            mm(out, kr[:, k, t * P:(t + 1) * P], gate_w[:, k, :], start=(k == 0), stop=False)
                        ins = mm(out, ones3[:, :], bias3[:, 3 * D:3 * D + E], start=False, stop=True)
                    done(ins, "gate")


DI, NS, DC, DR = 512, 16, 4, 16
KI = DI // P
JOBS_M = [("in", j) for j in range(2 * KI)] + [("bc",), ("dr",)] + [("dt", m) for m in range(KI)]


def phase_m(nc, g):
    ring = Ring(JOBS_M, 3)
    with ExitStack() as ctx:
        def sb(name, shape, dt=F32):
            return ctx.enter_context(nc.sbuf_tensor(name, shape, dt))

        def sem(name):
            return ctx.enter_context(nc.semaphore(name))

        w_in = sb("mw_in", [P, KD, 2 * DI])
        w_bc = sb("mw_bc", [P, KI, 3, 2 * NS])
        w_dr = sb("mw_dr", [P, KI, DR])
        w_dt = sb("mw_dt", [DR, DI])
        w_out = sb("mw_out", [P, KI, D])
        acol = sb("acol", [P, KI, NS])
        taps = sb("taps", [P, KI, DC])
        vecs = sb("vecs", [P, 3, KI])
        one = sb("one", [P, 1])
        pick = sb("pick", [3 * 2 * NS, 2 * NS, P], BF16)
        ident = sb("ident_m", [P, P])

        xT = sb("m_xT", [P, KD, L])
        xi = sb("m_xi", [P, KI, DC - 1 + L])
        zs = sb("m_zs", [P, KI * L])
        u = sb("m_u", [P, KI * L])
        dt = sb("m_dt", [P, KI * L])
        du = sb("m_du", [P, KI * L])
        bcs = sb("m_bcs", [3 * 2 * NS, L], BF16)
        bc2 = sb("m_bc2", [3 * 2 * NS, L], BF16)
        bcr = sb("m_bcr", [3 * 2 * NS, L])
        dr = sb("m_dr", [DR, L])
        sp_e = sb("m_spe", [P, L])
        sp_l = sb("m_spl", [P, L])
        dA = sb("m_dA", [P, 2, L])
        dB = sb("m_dB", [P, 2, L])
        h = sb("m_h", [P, 2, L])
        pr = sb("m_pr", [P, 2, L])
        yT = sb("m_yT", [P, KI * L])
        so = sb("m_so", [P, TB, D])

        W = [ctx.enter_context(nc.psum_tensor(f"m_work{i}", [P, 2 * CH], F32)) for i in range(3)]
        X = W[2]
        b_slot = lambda s: W[2 * s % 3]
        c_slot = lambda s: W[(2 * s + 1) % 3]
        Y = ctx.enter_context(nc.psum_tensor("m_Y", [P, 2 * CH], F32))

        w_ok = sem("m_w_in"); prep = sem("m_prep"); x_in = sem("m_x_in"); stored = sem("m_stored")
        full = [sem(f"m_full{i}") for i in range(3)]
        xi_ok = sem("m_xi_ok"); z_ok = sem("m_z_ok"); chain = sem("m_chain"); conv_ok = sem("m_conv_ok"); u_ok = sem("m_u_ok")
        dr_ok = sem("m_dr_ok"); bcs_ok = sem("m_bcs_ok"); bch = sem("m_bch"); sps = sem("m_sps"); sp_ok = sem("m_sp_ok")
        dt_ok = sem("m_dt_ok"); du_ok = sem("m_du_ok")
        b_full = sem("m_b_full"); c_full = sem("m_c_full"); dA_ok = sem("m_dA_ok"); dB_ok = sem("m_dB_ok")
        h_ok = sem("m_h_ok"); pr_ok = sem("m_pr_ok"); pr_used = sem("m_pr_used")
        y_ok = sem("m_y_ok"); yg_ok = sem("m_yg_ok"); o_full = sem("m_o_full"); o_ok = sem("m_o_ok")

        READ = {("bc",): (bch, 5, 2), ("dr",): (dr_ok, 1, 1)}
        for m in range(KI):
            READ["in", m] = (xi_ok, KI, m + 1)
            READ["in", KI + m] = (z_ok, KI, m + 1)
            READ["dt", m] = (dt_ok, 2 * KI, 2 * m + 1)

        def slot(*job):
            return W[ring.of[job][0]]

        def wait_full(e, b, *job):
            s, use = ring.of[job]
            e.wait_ge(full[s], b * ring.uses[s] + use + 1)

        def wait_slot(e, b, *job):
            at = JOBS_M.index(job)
            if at >= 3:
                s, per, k = READ[JOBS_M[at - 3]]
                e.wait_ge(s, b * per + k)

        LOADS = 14
        with nc.Block() as block:
            @block.sync
            def _(sp):
                def load(dst, src):
                    sp.dma_start(dst, src).then_inc(w_ok, 16)

                load(w_in[:, :, :], g["W_inT"].rearrange("(k p) n -> p k n", p=P))
                with nc.allow_non_contiguous_dma(reason="small weights, once"):
                    for i in range(3):
                        load(w_bc[:, :, i, :], g["W_xprojT"][:, DR:].rearrange("(k p) n -> p k n", p=P))
                    load(w_dr[:, :, :], g["W_xprojT"][:, 0:DR].rearrange("(k p) n -> p k n", p=P))
                    load(w_dt[:, :], g["W_dtT"])
                    load(w_out[:, :, :], g["W_outT"].rearrange("(k p) n -> p k n", p=P))
                    load(acol[:, :, :], g["A_log"].rearrange("(k p) n -> p k n", p=P))
                    load(taps[:, :, :], g["conv_w"].rearrange("(k p) n -> p k n", p=P))
                    for i, n in enumerate(("conv_b", "b_dt", "D_skip")):
                        load(vecs[:, i, :], g[n].rearrange("(k p) -> p k", p=P))
                    load(ident[:, :], g["ident"])
                    load(sp_l[:, :], g["xn1T_s"][0][:, 0, :])
                sp.dma_start(xT[:, :, :], g["xn1T_s"][0]).then_inc(x_in, 16)

                def batch(b, last):
                    if not last:
                        sp.wait_ge(z_ok, b * KI + KI)
                        sp.dma_start(xT[:, :, :], g["xn1T_s"][b + 1]).then_inc(x_in, 16)
                    sp.wait_ge(o_ok, b * 2 + 2)
                    sp.dma_start(g["m_s"][b].rearrange("(t p) d -> p t d", p=P), so[:, :, :]).then_inc(stored, 16)

                with sp.Fori(0, B - 1) as b:
                    batch(b, False)
                batch(B - 1, True)
                sp.wait_ge(stored, 16 * B)

            @block.gpsimd
            def _(pool):
                nc.gpsimd.memset(xi[:, :, 0:DC - 1], 0.0).then_inc(prep, 1)
                nc.gpsimd.memset(one[:, :], 1.0).then_inc(prep, 1)
                nc.gpsimd.memset(pick[:, :, :], 0.0).then_inc(prep, 1)
                for i in range(3):
                    pool.wait_ge(prep, 3 + i)
                    nc.gpsimd.affine_select(out=pick[:, :, :], in_=pick[:, :, :], compare_op=ALU.not_equal, fill=1.0, base=-2 * NS * i,
                                            pattern=[[-1, 2 * NS], [0, P]], channel_multiplier=1).then_inc(prep, 1)
                with pool.Fori(0, B) as b:
                    for m in range(KI):
                        pool.wait_ge(dt_ok, b * 2 * KI + 2 * m + 2)
                        nc.gpsimd.tensor_tensor(du[:, m * L:(m + 1) * L], dt[:, m * L:(m + 1) * L], u[:, m * L:(m + 1) * L],
                                                ALU.mult).then_inc(du_ok, 1)

            @block.scalar
            def _(ac):
                A = nc.scalar.activation
                ac.wait_ge(w_ok, 16 * LOADS)
                ac.wait_ge(prep, 6)
                A(acol[:, :, :], acol[:, :, :], ACT.Exp).then_inc(prep, 1)
                ac.wait_ge(prep, 8)
                with ac.Fori(0, B) as b:
                    for m in range(KI):
                        wait_full(ac, b, "in", m)
                        A(xi[:, m, DC - 1:], slot("in", m)[:, :], ACT.Identity).then_inc(xi_ok, 1)
                    for m in range(KI):
                        wait_full(ac, b, "in", KI + m)
                        A(zs[:, m * L:(m + 1) * L], slot("in", KI + m)[:, :], ACT.Silu).then_inc(z_ok, 1)
                    for m in range(KI):
                        ac.wait_ge(conv_ok, b * KI + m + 1)
                        A(u[:, m * L:(m + 1) * L], u[:, m * L:(m + 1) * L], ACT.Silu).then_inc(u_ok, 1)
                    wait_full(ac, b, "dr")
                    A(dr[:, :], slot("dr")[0:DR, :], ACT.Identity).then_inc(dr_ok, 1)
                    for m in range(KI):
                        wait_full(ac, b, "dt", m)
                        if m:
                            ac.wait_ge(sp_ok, b * KI + m)
                        A(sp_e[:, :], slot("dt", m)[:, :], ACT.Abs, bias=vecs[:, 1, m:m + 1]).then_inc(sps, 1)
                        ac.wait_ge(sps, b * 2 * KI + 2 * m + 1)
                        A(sp_e[:, :], sp_e[:, :], ACT.Exp, scale=-1.0).then_inc(sps, 1)
                        ac.wait_ge(sps, b * 2 * KI + 2 * m + 2)
                        if m:
                            ac.wait_ge(dt_ok, b * 2 * KI + 2 * m)
                        A(sp_l[:, :], sp_e[:, :], ACT.Ln, bias=one[:, :]).then_inc(sp_ok, 1)
                    with ac.Fori(0, KI) as m:
                        n = b * KI + m
                        for s in range(NS):
                            ac.wait_ge(h_ok, n * NS + s + 1)
                            A(dA[:, s % 2, :], dt[:, bass.ds(m * L, L)], ACT.Exp, scale=acol[:, bass.ds(m, 1), s]).then_inc(dA_ok, 1)

            @block.vector
            def _(dv):
                v_ = nc.vector
                dv.wait_ge(prep, 7)
                v_.tensor_scalar(acol[:, :, :], acol[:, :, :], -1.0, None, ALU.mult).then_inc(prep, 1)
                v_.memset(h[:, 0, 0:1], 0.0).then_inc(y_ok, 1)
                dv.wait_ge(y_ok, 1)
                v_.memset(dB[:, 0, 0:1], 0.0).then_inc(dB_ok, 1)
                v_.memset(pr[:, 0, 0:1], 0.0).then_inc(pr_ok, 1)
                dv.wait_ge(dB_ok, 1)
                dv.wait_ge(pr_ok, 1)
                for i in range(2):
                    v_.memset(h[:, i, 1:2], 0.0).then_inc(h_ok, 1)
                with dv.Fori(0, B) as b:
                    n_ = [0]

                    def link(k):
                        n_[0] += k
                        dv.wait_ge(chain, b * 3 * KI + n_[0])

                    for m in range(KI):
                        um = u[:, m * L:(m + 1) * L]
                        dv.wait_ge(xi_ok, b * KI + m + 1)
                        v_.tensor_scalar(um, xi[:, m, 0:L], taps[:, m, 0:1], vecs[:, 0, m:m + 1], ALU.mult, ALU.add).then_inc(chain, 1)
                        link(1)
                        for k in range(1, DC):
                            i = v_.scalar_tensor_tensor(um, xi[:, m, k:k + L], taps[:, m, k:k + 1], um, ALU.mult, ALU.add)
                            if k < DC - 1:
                                i.then_inc(chain, 1)
                                link(1)
                            else:
                                i.then_inc(conv_ok, 1)
                    wait_full(dv, b, "bc")
                    v_.tensor_copy(bcs[:, :], slot("bc")[0:96, :]).then_inc(bch, 1)
                    dv.wait_ge(bch, b * 5 + 1)
                    v_.tensor_tensor(bcr[:, :], slot("bc")[0:96, :], bcs[:, :], ALU.subtract).then_inc(bch, 1)
                    dv.wait_ge(bch, b * 5 + 2)
                    v_.tensor_copy(bc2[:, :], bcr[:, :]).then_inc(bch, 1)
                    dv.wait_ge(bch, b * 5 + 3)
                    v_.tensor_tensor(bcr[:, :], bcr[:, :], bc2[:, :], ALU.subtract).then_inc(bch, 1)
                    v_.tensor_copy(bcs[32:64, :], bc2[32:64, :]).then_inc(bch, 1)
                    dv.wait_ge(bch, b * 5 + 5)
                    v_.tensor_copy(bcs[64:96, :], bcr[64:96, :]).then_inc(bcs_ok, 1)
                    for m in range(KI):
                        dm = dt[:, m * L:(m + 1) * L]
                        dv.wait_ge(sps, b * 2 * KI + 2 * m + 1)
                        v_.tensor_scalar(dm, slot("dt", m)[:, :], vecs[:, 1, m:m + 1], 0.0, ALU.add, ALU.max).then_inc(dt_ok, 1)
                        dv.wait_ge(dt_ok, b * 2 * KI + 2 * m + 1)
                        dv.wait_ge(sp_ok, b * KI + m + 1)
                        v_.tensor_tensor(dm, dm, sp_l[:, :], ALU.add).then_inc(dt_ok, 1)
                    with dv.Fori(0, KI) as m:
                        n = b * KI + m
                        dv.wait_ge(du_ok, b * KI + KI)

                        def times_b(s):
                            dv.wait_ge(b_full, n * NS + s + 1)
                            v_.tensor_tensor(dB[:, s % 2, :], du[:, bass.ds(m * L, L)], b_slot(s)[:, :], ALU.mult).then_inc(dB_ok, 1)

                        times_b(0)
                        for s in range(NS):
                            dv.wait_ge(dB_ok, n * NS + s + 2)
                            dv.wait_ge(dA_ok, n * NS + s + 1)
                            v_.tensor_tensor_scan(h[:, s % 2, :], dA[:, s % 2, :], dB[:, s % 2, :], 0.0, ALU.mult, ALU.add).then_inc(h_ok, 1)
                            if s < NS - 1:
                                times_b(s + 1)
                            dv.wait_ge(h_ok, n * NS + s + 3)
                            dv.wait_ge(c_full, n * NS + s + 1)
                            if s >= 2:
                                dv.wait_ge(pr_used, n * NS + s - 1)
                            v_.tensor_tensor(pr[:, s % 2, :], h[:, s % 2, :], c_slot(s)[:, :], ALU.mult).then_inc(pr_ok, 1)
                        dv.wait_ge(pr_used, n * NS + NS)
                        v_.scalar_tensor_tensor(yT[:, bass.ds(m * L, L)], u[:, bass.ds(m * L, L)], vecs[:, 2, bass.ds(m, 1)], Y[:, :],
                                                ALU.mult, ALU.add).then_inc(y_ok, 1)
                        dv.wait_ge(y_ok, n + 2)
                        v_.tensor_tensor(yT[:, bass.ds(m * L, L)], yT[:, bass.ds(m * L, L)], zs[:, bass.ds(m * L, L)], ALU.mult).then_inc(yg_ok, 1)
                    if True:
                        for i, o in enumerate((X, Y)):
                            dv.wait_ge(o_full, b * 2 + i + 1)
                            if i == 0:
                                dv.wait_ge(z_ok, b * KI + KI)
                            v_.tensor_copy(so[:, 4 * i:4 * i + 4, :].rearrange("p t d -> p (t d)"), o[:, :]).then_inc(o_ok, 1)
                        dv.wait_ge(stored, b * 16 + 16)

            @block.tensor
            def _(pe):
                mm = nc.tensor.matmul
                pe.wait_ge(w_ok, 16 * LOADS)
                pe.wait_ge(prep, 6)

                def done(ins, *job):
                    ins.then_inc(full[ring.of[job][0]], 1)

                with pe.Fori(0, B) as b:
                    pe.wait_ge(x_in, b * 16 + 16)
                    for j in range(2 * KI):
                        wait_slot(pe, b, "in", j)
                        for c in range(NC_):
                            for k in range(KD):
                                ins = mm(slot("in", j)[:, c * CH:(c + 1) * CH], w_in[:, k, j * P:(j + 1) * P], xT[:, k, c * CH:(c + 1) * CH],
                                         start=(k == 0), stop=(k == KD - 1))
                        done(ins, "in", j)
                    pe.wait_ge(u_ok, b * KI + KI)
                    for job, w, rows in ((("bc",), w_bc[:, :, :, :].rearrange("p k i n -> p k (i n)"), 96), (("dr",), w_dr, DR)):
                        wait_slot(pe, b, *job)
                        for c in range(NC_):
                            for k in range(KI):
                                ins = mm(slot(*job)[0:rows, c * CH:(c + 1) * CH], w[:, k, :], u[:, k * L + c * CH:k * L + (c + 1) * CH],
                                         start=(k == 0), stop=(k == KI - 1))
                        done(ins, *job)
                    pe.wait_ge(dr_ok, b + 1)
                    for m in range(KI):
                        wait_slot(pe, b, "dt", m)
                        for c in range(NC_):
                            ins = mm(slot("dt", m)[:, c * CH:(c + 1) * CH], w_dt[:, m * P:(m + 1) * P], dr[:, c * CH:(c + 1) * CH],
                                     start=True, stop=True)
                        done(ins, "dt", m)
                    with pe.Fori(0, KI) as m:
                        n = b * KI + m

                        def spread(dst, row, ok):
                            for c in range(NC_):
                                ins = mm(dst[:, c * CH:(c + 1) * CH], pick[:, row, :], bcs[:, c * CH:(c + 1) * CH], start=True, stop=True)
                            ins.then_inc(ok, 1)

                        def add_state(s):
                            if s == 0:
                                pe.wait_ge(y_ok, n + 1)
                            for c in range(NC_):
                                ins = mm(Y[:, c * CH:(c + 1) * CH], ident[:, :], pr[:, s % 2, c * CH:(c + 1) * CH],
                                         start=(s == 0), stop=(s == NS - 1), skip_group_check=True)
                            ins.then_inc(pr_used, 1)

                        pe.wait_ge(bcs_ok, b + 1)
                        pe.wait_ge(dt_ok, b * 2 * KI + 2 * KI)
                        pe.wait_ge(dB_ok, n * NS + 1)
                        spread(b_slot(0), 0, b_full)
                        pe.wait_ge(pr_ok, n * NS + 1)
                        spread(c_slot(0), NS, c_full)
                        for s in range(NS):
                            if s < NS - 1:
                                if s:
                                    pe.wait_ge(pr_ok, n * NS + s + 1)
                                spread(b_slot(s + 1), s + 1, b_full)
                                pe.wait_ge(dB_ok, n * NS + s + 2)
                                spread(c_slot(s + 1), NS + s + 1, c_full)
                            if s:
                                if s == NS - 1:
                                    pe.wait_ge(pr_ok, n * NS + s + 1)
                                add_state(s - 1)
                        pe.wait_ge(pr_ok, n * NS + NS + 1)
                        add_state(NS - 1)
                    pe.wait_ge(yg_ok, b * KI + KI)
                    for i, o in enumerate((X, Y)):
                        for t in range(4):
                            for k in range(KI):
                                at = k * L + (4 * i + t) * P
                                ins = mm(o[:, t * D:(t + 1) * D], yT[:, at:at + P], w_out[:, k, :], start=(k == 0), stop=(k == KI - 1))
                        ins.then_inc(o_full, 1)
                    pe.wait_ge(o_ok, b * 2 + 2)


NTILE = 40
S = NTILE * P
GROUP = 5


def phase_e(nc, g):
    with ExitStack() as ctx:
        def sb(name, shape, dt=F32):
            return ctx.enter_context(nc.sbuf_tensor(name, shape, dt))

        def sem(name):
            return ctx.enter_context(nc.semaphore(name))

        def ps(name, shape):
            return ctx.enter_context(nc.psum_tensor(name, shape, F32))

        lg = g["lg"]
        ROUTE_OH = []
        e_w1 = sb("e_w1", [P, KD, E * HE])
        e_w2 = sb("e_w2", [P, HE // P, E * D])
        brow = sb("e_brow", [1, E * (HE + D)])
        brs = sb("e_brs", [1, E * (HE + D)])
        bsp = sb("e_bsp", [1, E * (HE + D)], BF16)
        bias3 = sb("e_bias3", [3, E * (HE + D)], BF16)
        ones3 = sb("e_ones3", [3, P], BF16)
        ident = sb("ident_e", [P, P])
        tri = sb("tri", [P, P])
        ones = sb("ones_e", [P, P])
        eidx_i = sb("eidx_i", [P, NT, E], I32)
        eidx = sb("eidx", [P, NT, E])
        jidx_i = sb("jidx_i", [P, NTILE, E], I32)
        jidx = sb("jidx", [P, NTILE, E])
        keep = sb("keep", [P, E, NT])
        one8 = sb("one8", [P, E])
        gamma = sb("gamma", [P, 2, D])

        m8 = sb("m8", [P, NT]); ex = sb("ex", [P, NT, E])
        srt = sb("srt", [P, NT, 8]); srti = sb("srti", [P, NT, 8], mybir.dt.uint32)
        idf = sb("idf", [P, NT, 2])
        oh = sb("oh", [P, NT, E]); tot = sb("tot", [P, E, NT]); inc = sb("inc", [P, E, NT]); a8 = sb("a8", [P, NT, E])
        cnt = sb("cnt", [P, 4, E])
        jge = sb("jge", [P, NTILE, E]); jf = sb("jf", [P, NTILE])
        posf = sb("posf", [P, 1, NT]); pos = sb("pos", [P, 2, NT], I32)
        texp = sb("texp", [P, 2, NTILE], I32)

        spare = sb("e_spare", [P, 16])
        zero = sb("zero", [P, D])
        tok = sb("tok", [P, 4, D]); got = sb("got", [P, 4, D]); part = sb("part", [P, 4, D])
        ix = sb("ix", [P, 4, 2], I32); vv = sb("vv", [P, 4, 2])
        xs = sb("xs", [P, GROUP, D]); xsT = sb("xsT", [P, KD, P]); hs = sb("hs", [P, HE])
        hT = sb("hT", [P, HE // P, P]); ys = sb("ys", [P, GROUP, D])
        ms = sb("ms", [P, 4, D]); x1 = sb("x1t", [P, 4, D])
        st = sb("st_e", [P, 4, 6]); mv = sb("mv_e", [P, 4, 2]); rs = sb("rs_e", [P, 4, 4])
        X0 = ps("eX0", [P, CH]); X1 = ps("eX1", [P, CH])

        w_ok = sem("e_w_ok"); c_ok = sem("e_const"); bs = sem("e_bias_split"); b_in = sem("e_bias_in")
        rt = sem("e_route"); rt_pe = sem("e_route_pe"); rt_act = sem("e_route_act"); rt_ok = sem("e_route_ok")
        zeroed = sem("e_zeroed"); tok_in = sem("e_tok_in"); sc = sem("e_scattered"); ix_ok = sem("e_ix_ok")
        bo = sem("e_boost"); disp = sem("e_dispatch"); got_in = sem("e_got_in"); part_out = sem("e_part_out")
        xs_in = [sem(f"e_xs_in{i}") for i in range(GROUP)]; t1 = sem("e_t1"); t1c = sem("e_t1c"); m1 = sem("e_m1"); m1c = sem("e_m1c")
        t2 = sem("e_t2"); t2c = sem("e_t2c"); m2 = sem("e_m2"); m2c = sem("e_m2c"); ys_out = [sem(f"e_ys_out{i}") for i in range(GROUP)]
        f_in = sem("e_f_in"); f_dve = sem("e_f_dve"); f_act = sem("e_f_act"); f_out = sem("e_f_out"); f_ok = sem("e_f_ok"); f_got = sem("e_f_got")
        NQ = NT // 4
        NG = NTILE // GROUP
        LOADS = 5 + 2 * E
        FD = 1 + 4 + 4 + 2 + 3 + 16 + 4 + 2 + 1
        RD = 3 + 4
        tokens = lambda ap: ap.rearrange("(t p) d -> p t d", p=P)
        xn1_q = g["xn1_s"].rearrange("b (c n) d -> (b c) n d", n=4 * P)
        x1_q = g["x1_s"].rearrange("b (c n) d -> (b c) n d", n=4 * P)
        m_q = g["m_s"].rearrange("b (c n) d -> (b c) n d", n=4 * P)
        out_q = g["out"].rearrange("b (c n) d -> (b c) n d", n=4 * P)

        with nc.Block() as block:
            @block.sync
            def _(sp):
                def load(dst, src):
                    sp.dma_start(dst, src).then_inc(w_ok, 16)

                load(brow[:, 0:E * HE], g["e_b1"].rearrange("e n -> (e n)").rearrange("(a n) -> a n", a=1))
                load(brow[:, E * HE:], g["e_b2"].rearrange("e n -> (e n)").rearrange("(a n) -> a n", a=1))
                load(ident[:, :], g["ident"])
                for i, n in enumerate(("ln_gamma", "ln_beta")):
                    load(gamma[:, i, :], g[n].rearrange("(a n) -> a n", a=1).to_broadcast([P, D]))
                for e in range(E):
                    load(e_w1[:, :, e * HE:(e + 1) * HE], g["e_W1"][e].rearrange("(k p) n -> p k n", p=P))
                    load(e_w2[:, :, e * D:(e + 1) * D], g["e_W2"][e].rearrange("(k p) n -> p k n", p=P))
                for i in range(3):
                    sp.wait_ge(bs, 2 * i + 1)
                    if i:
                        sp.wait_ge(b_in, 16 * i)
                    sp.dma_start(bias3[i:i + 1, :], bsp[:, :]).then_inc(b_in, 16)
                sp.wait_ge(c_ok, 1)
                with sp.Fori(0, NTILE) as j:
                    sp.dma_start(g["xs_s"][bass.ds(j * P, P), :], zero[:, :]).then_inc(zeroed, 16)
                for r in range(2):

                    def group(q, first=False):
                        if not first:
                            sp.wait_ge(sc, (r * NQ + q) * 64)
                        sp.dma_start(tok[:, :, :], tokens(xn1_q[q])).then_inc(tok_in, 16)
                        if r:
                            sp.wait_ge(bo, q * 2 + 2)
                            sp.dma_start(tokens(g["part_s"][q]), part[:, :, :]).then_inc(part_out, 16)

                    group(0, first=not r)
                    with sp.Fori(1, NQ) as q:
                        group(q)
                    sp.wait_ge(sc, (r + 1) * NT * 16)

                    def load_xs(q, i):
                        sp.wait_ge(t1, (r * NG + q) * GROUP + i + 1)
                        sp.dma_start(xs[:, i, :], g["xs_s"][bass.ds((q * GROUP + i) * P, P), :]).then_inc(xs_in[i], 16)

                    def turn(q, last):
                        for i in range(GROUP):
                            n = (r * NG + q) * GROUP + i
                            sp.wait_ge(m2c, n + 2)
                            sp.dma_start(g[f"y{r}_s"][bass.ds((q * GROUP + i) * P, P), :], ys[:, i, :]).then_inc(ys_out[i], 16)
                            if not last:
                                load_xs(q + 1, i)

                    for i in range(GROUP):
                        load_xs(0, i)
                    with sp.Fori(0, NG - 1) as q:
                        turn(q, False)
                    turn(NG - 1, True)
                with sp.Fori(0, NQ) as q:
                    sp.wait_ge(f_out, q * 16 + 1)
                    sp.dma_start(part[:, :, :], tokens(g["part_s"][q])).then_inc(f_in, 16)
                    sp.dma_start(ms[:, :, :], tokens(m_q[q])).then_inc(f_in, 16)
                    sp.dma_start(x1[:, :, :], tokens(x1_q[q])).then_inc(f_in, 16)
                    sp.wait_ge(f_ok, q + 1)
                    sp.dma_start(tokens(out_q[q]), x1[:, :, :]).then_inc(f_out, 16)
                sp.wait_ge(f_out, NQ * 16 + 1)
                sp.wait_ge(part_out, NQ * 16)

            @block.gpsimd
            def _(pool):
                nc.gpsimd.memset(zero[:, :], 0.0).then_inc(c_ok, 1)
                nc.gpsimd.memset(ones[:, :], 1.0).then_inc(c_ok, 1)
                nc.gpsimd.memset(one8[:, :], 1.0).then_inc(c_ok, 1)
                nc.gpsimd.memset(ones3[:, :], 1.0).then_inc(c_ok, 1)
                nc.gpsimd.memset(keep[:, :, :], 1.0).then_inc(c_ok, 1)
                nc.gpsimd.iota(eidx_i[:, :, :], pattern=[[0, NT], [1, E]], base=0, channel_multiplier=0).then_inc(c_ok, 1)
                nc.gpsimd.iota(jidx_i[:, :, :], pattern=[[1, NTILE], [0, E]], base=0, channel_multiplier=0).then_inc(c_ok, 1)
                pool.wait_ge(c_ok, 7)
                nc.gpsimd.memset(keep[:, :, 0:1], 0.0).then_inc(c_ok, 1)
                nc.gpsimd.affine_select(out=tri[:, :], in_=ones[:, :], compare_op=ALU.is_gt, fill=0.0, base=0,
                                        pattern=[[1, P]], channel_multiplier=-1).then_inc(c_ok, 1)
                pool.wait_ge(rt_ok, 1)
                pool.wait_ge(zeroed, NTILE * 16)

                def rows(table, i, k):
                    return table, bass.IndirectOffsetOnAxis(ap=ix[:, i, k:k + 1], axis=0)

                for r in range(2):
                    if r:
                        for i in range(GROUP):
                            pool.wait_ge(ys_out[i], 16 * NG + 16)
                    for q in range(NQ):
                        n = r * NQ + q
                        pool.wait_ge(ix_ok, n + 1)
                        if r:
                            for i in range(4):
                                nc.gpsimd.indirect_dma_start(got[:, i, :], None, *rows(g["y0_s"], i, 0)).then_inc(got_in, 16)
                            pool.wait_ge(bo, q * 2 + 2)
                        else:
                            pool.wait_ge(tok_in, n * 16 + 16)
                        for i in range(4):
                            nc.gpsimd.indirect_dma_start(*rows(g["xs_s"], i, r), tok[:, i, :], None).then_inc(sc, 16)
                for i in range(GROUP):
                    pool.wait_ge(ys_out[i], 16 * 2 * NG + 16)
                for q in range(NQ):
                    pool.wait_ge(ix_ok, 2 * NQ + q + 1)
                    for i in range(4):
                        nc.gpsimd.indirect_dma_start(got[:, i, :], None, *rows(g["y1_s"], i, 1)).then_inc(f_got, 16)

            @block.scalar
            def _(ac):
                A = nc.scalar.activation
                ac.wait_ge(rt, 2)
                A(ex[:, :, :], ex[:, :, :], ACT.Exp).then_inc(rt_act, 1)
                for r in range(2):
                    with ac.Fori(0, NG) as q:
                        for i in range(GROUP):
                            n = (r * NG + q) * GROUP + i
                            ac.wait_ge(t1, n + GROUP + 1)
                            A(xsT[:, :, :].rearrange("p k t -> p (k t)"), X0[:, 0:D], ACT.Identity).then_inc(t1c, 1)
                            ac.wait_ge(m1, n + 1)
                            A(hs[:, :], X1[:, :], ACT.Relu).then_inc(m1c, 1)
                            ac.wait_ge(t2, n + 1)
                            A(hT[:, :, :].rearrange("p k t -> p (k t)"), X0[:, :], ACT.Identity).then_inc(t2c, 1)
                            ac.wait_ge(m2, n + 1)
                            ac.wait_ge(ys_out[i], 16 * (r * NG + q) + 16)
                            A(ys[:, i, :], X1[:, 0:D], ACT.Identity).then_inc(m2c, 1)
                with ac.Fori(0, NQ) as q:
                    ac.wait_ge(f_dve, q * FD + FD - 1)
                    A(got[:, :, :], got[:, :, :], ACT.Silu).then_inc(f_act, 1)

            @block.vector
            def _(dv):
                v_ = nc.vector
                k = [0]

                def step(ins):
                    ins.then_inc(rt, 1)
                    k[0] += 1
                    dv.wait_ge(rt, k[0])

                over_e = lambda ap, n: ap.unsqueeze(2).to_broadcast([P, n, E])
                over_t = lambda ap, n: ap.unsqueeze(1).to_broadcast([P, n, E])
                step(v_.tensor_reduce(m8[:, :], lg[:, :, :], AX.X, ALU.max))
                step(v_.tensor_tensor(ex[:, :, :], lg[:, :, :], over_e(m8[:, :], NT), ALU.subtract))
                dv.wait_ge(rt_act, 1)
                step(v_.tensor_reduce(m8[:, :], ex[:, :, :], AX.X, ALU.add))
                step(v_.reciprocal(m8[:, :], m8[:, :]))
                step(v_.tensor_tensor(ex[:, :, :], ex[:, :, :], over_e(m8[:, :], NT), ALU.mult))
                for t in range(NT):
                    v_.max(srt[:, t, :], ex[:, t, :]).then_inc(rt, 1)
                k[0] += NT
                dv.wait_ge(rt, k[0])
                for t in range(NT):
                    v_.max_index(srti[:, t, :], srt[:, t, :], ex[:, t, :]).then_inc(rt, 1)
                k[0] += NT
                dv.wait_ge(rt, k[0])
                step(v_.tensor_copy(idf[:, :, :], srti[:, :, 0:2]))
                dv.wait_ge(c_ok, 9)
                step(v_.tensor_copy(eidx[:, :, :], eidx_i[:, :, :]))
                step(v_.tensor_copy(jidx[:, :, :], jidx_i[:, :, :]))
                for r in range(2):
                    step(v_.tensor_tensor(oh[:, :, :], eidx[:, :, :], over_e(idf[:, :, r], NT), ALU.is_equal))
                    ROUTE_OH.append(k[0])
                    dv.wait_ge(rt_pe, 2 * r + 2)
                    step(v_.tensor_copy(tot[:, :, :], X1[:, 0:NT * E].rearrange("p (t e) -> p e t", e=E)))
                    flat = lambda ap: ap.rearrange("p e t -> p (e t)")
                    step(v_.tensor_tensor_scan(flat(inc[:, :, :]), flat(keep[:, :, :]), flat(tot[:, :, :]), 0.0, ALU.mult, ALU.add))
                    step(v_.tensor_tensor(tot[:, :, :], inc[:, :, :], tot[:, :, :], ALU.subtract))
                    step(v_.tensor_scalar(cnt[:, 0, :], inc[:, :, NT - 1], 1.0 / P, (P / 2 - 0.5) / P, ALU.mult, ALU.add))
                    step(v_.tensor_scalar(cnt[:, 0, :], cnt[:, 0, :], ROUND, ROUND, ALU.add, ALU.subtract))
                    step(v_.tensor_tensor_scan(cnt[:, 1, :], one8[:, :], cnt[:, 0, :], 0.0, ALU.mult, ALU.add))
                    step(v_.tensor_tensor(cnt[:, 2, :], cnt[:, 1, :], cnt[:, 0, :], ALU.subtract))
                    step(v_.tensor_scalar(cnt[:, 2, :], cnt[:, 2, :], float(P), None, ALU.mult))
                    step(v_.tensor_tensor(a8[:, :, :], X0[:, 0:NT * E].rearrange("p (t e) -> p t e", e=E),
                                          tot[:, :, :].rearrange("p e t -> p t e"), ALU.add))
                    step(v_.tensor_tensor(a8[:, :, :], a8[:, :, :], over_t(cnt[:, 2, :], NT), ALU.add))
                    step(v_.tensor_tensor(a8[:, :, :], a8[:, :, :], oh[:, :, :], ALU.mult))
                    step(v_.tensor_reduce(posf[:, 0, :], a8[:, :, :], AX.X, ALU.add))
                    step(v_.tensor_copy(pos[:, r, :], posf[:, 0, :]))
                    step(v_.tensor_tensor(jge[:, :, :], jidx[:, :, :], over_t(cnt[:, 1, :], NTILE), ALU.is_ge))
                    step(v_.tensor_reduce(jf[:, :], jge[:, :, :], AX.X, ALU.add))
                    step(v_.tensor_scalar(jf[:, :], jf[:, :], float(E - 1), None, ALU.min))
                    step(v_.tensor_copy(texp[:, r, :], jf[:, :]))
                dv.wait_ge(w_ok, 16 * LOADS)
                src = brow
                for i in range(3):
                    if i:
                        dv.wait_ge(b_in, 16 * i)
                    v_.tensor_copy(bsp[:, :], src[:, :]).then_inc(bs, 1)
                    dv.wait_ge(bs, 2 * i + 1)
                    v_.tensor_tensor(brs[:, :], src[:, :], bsp[:, :], ALU.subtract).then_inc(bs, 1)
                    dv.wait_ge(bs, 2 * i + 2)
                    src = brs
                for i, (s, n) in enumerate(((t1, GROUP), (t2c, 1), (m2c, 1), (f_out, 1), (rt_ok, 1)) + tuple((s, 16) for s in ys_out)):
                    v_.memset(spare[:, i:i + 1], 0.0).then_inc(s, n)
                v_.tensor_copy(ix[:, :, 0], pos[:, 0, 0:4]).then_inc(ix_ok, 1)
                with dv.Fori(1, NQ) as q:
                    dv.wait_ge(sc, q * 64)
                    v_.tensor_copy(ix[:, :, 0], pos[:, 0, bass.ds(q * 4, 4)]).then_inc(ix_ok, 1)
                with dv.Fori(0, NQ) as q:
                    dv.wait_ge(sc, (NQ + q) * 64)
                    v_.tensor_copy(ix[:, :, 0], pos[:, 0, bass.ds(q * 4, 4)]).then_inc(disp, 1)
                    v_.tensor_copy(ix[:, :, 1], pos[:, 1, bass.ds(q * 4, 4)]).then_inc(disp, 1)
                    v_.tensor_copy(vv[:, :, 0], srt[:, bass.ds(q * 4, 4), 0]).then_inc(disp, 1)
                    dv.wait_ge(disp, q * RD + 3)
                    v_.memset(spare[:, 15:16], 0.0).then_inc(ix_ok, 1)
                    dv.wait_ge(tok_in, (NQ + q) * 16 + 16)
                    dv.wait_ge(got_in, q * 64 + 64)
                    for i in range(4):
                        v_.scalar_tensor_tensor(part[:, i, :], got[:, i, :], vv[:, i, 0:1], tok[:, i, :], ALU.mult, ALU.add).then_inc(disp, 1)
                    dv.wait_ge(disp, q * RD + RD)
                    dv.wait_ge(ix_ok, NQ + q + 1)
                    v_.scalar_tensor_tensor(tok[:, :, :].rearrange("p t d -> p (t d)"), got[:, :, :].rearrange("p t d -> p (t d)"), 0.5,
                                            tok[:, :, :].rearrange("p t d -> p (t d)"), ALU.mult, ALU.add).then_inc(bo, 2)
                    dv.wait_ge(bo, q * 2 + 2)
                    dv.wait_ge(part_out, q * 16 + 16)
                dv.wait_ge(sc, 2 * NT * 16)
                with dv.Fori(0, NQ) as q:
                    c = [0]

                    def link(n):
                        c[0] += n
                        dv.wait_ge(f_dve, q * FD + c[0])

                    v_.tensor_copy(vv[:, :, 1], srt[:, bass.ds(q * 4, 4), 1]).then_inc(f_dve, 1)
                    v_.tensor_copy(ix[:, :, 1], pos[:, 1, bass.ds(q * 4, 4)]).then_inc(ix_ok, 1)
                    link(1)
                    dv.wait_ge(f_in, q * 48 + 48)
                    dv.wait_ge(f_got, q * 64 + 64)
                    for i in range(4):
                        v_.scalar_tensor_tensor(got[:, i, :], got[:, i, :], vv[:, i, 1:2], part[:, i, :], ALU.mult, ALU.add).then_inc(f_dve, 1)
                    link(4)
                    for i in range(4):
                        v_.bn_stats(st[:, i, :], got[:, i, :]).then_inc(f_dve, 1)
                    link(4)
                    v_.memset(spare[:, 14:15], 0.0).then_inc(f_dve, 1)
                    for i in range(4):
                        i_ = v_.bn_aggr(mv[:, i, :], st[:, i, :])
                        if i == 3:
                            i_.then_inc(f_dve, 1)
                    link(2)
                    var, y, y2, hh = (rs[:, i, :] for i in range(4))
                    for i_ in (lambda: v_.tensor_scalar(var, mv[:, :, 1], EPS, None, ALU.add),
                               lambda: v_.tensor_scalar(hh.bitcast(I32), var.bitcast(I32), 1, None, ALU.logical_shift_right),
                               lambda: v_.tensor_scalar(y.bitcast(I32), hh.bitcast(I32), -1.0, RSQRT_SEED, ALU.mult, ALU.add)):
                        i_().then_inc(f_dve, 1)
                        link(1)
                    for _ in range(4):
                        for i_ in (lambda: v_.tensor_tensor(y2, y, y, ALU.mult), lambda: v_.tensor_tensor(y2, y2, var, ALU.mult),
                                   lambda: v_.tensor_scalar(y2, y2, -0.5, 1.5, ALU.mult, ALU.add), lambda: v_.tensor_tensor(y, y, y2, ALU.mult)):
                            i_().then_inc(f_dve, 1)
                            link(1)
                    for i in range(4):
                        v_.tensor_scalar(got[:, i, :], got[:, i, :], mv[:, i, 0:1], y[:, i:i + 1], ALU.subtract, ALU.mult).then_inc(f_dve, 1)
                    link(4)
                    gb = lambda i: gamma[:, i, :].unsqueeze(1).to_broadcast([P, 4, D])
                    v_.tensor_tensor(got[:, :, :], got[:, :, :], gb(0), ALU.mult).then_inc(f_dve, 1)
                    link(1)
                    v_.tensor_tensor(got[:, :, :], got[:, :, :], gb(1), ALU.add).then_inc(f_dve, 1)
                    link(1)
                    dv.wait_ge(f_act, q + 1)
                    v_.tensor_tensor(got[:, :, :], got[:, :, :], ms[:, :, :], ALU.mult).then_inc(f_dve, 1)
                    link(1)
                    v_.tensor_tensor(x1[:, :, :], got[:, :, :], x1[:, :, :], ALU.add).then_inc(f_ok, 1)
                    dv.wait_ge(f_ok, q + 1)
                    assert c[0] == FD, (c[0], FD)

            @block.tensor
            def _(pe):
                mm = nc.tensor.matmul
                pe.wait_ge(c_ok, 9)
                for r in range(2):
                    pe.wait_ge(rt, ROUTE_OH[r])
                    flat = oh[:, :, :].rearrange("p t e -> p (t e)")
                    mm(X0[:, 0:NT * E], tri[:, :], flat, start=True, stop=True).then_inc(rt_pe, 1)
                    mm(X1[:, 0:NT * E], ones[:, :], flat, start=True, stop=True).then_inc(rt_pe, 1)
                pe.wait_ge(rt_ok, 1)
                pe.wait_ge(b_in, 48)
                pe.wait_ge(w_ok, 16 * LOADS)
                for r in range(2):
                    with pe.Fori(0, NG) as q:
                        for i in range(GROUP):
                            n = (r * NG + q) * GROUP + i
                            e = pe.value_load(texp[0:1, r, bass.ds(q * GROUP + i, 1)], min_val=0, max_val=E - 1)
                            pe.wait_ge(xs_in[i], (r * NG + q) * 16 + 16)
                            pe.wait_ge(t2c, n + 1)
                            for k in range(KD):
                                ins = nc.tensor.transpose(X0[:, k * P:(k + 1) * P], xs[:, i, k * P:(k + 1) * P], ident[:, :])
                            ins.then_inc(t1, 1)
                            pe.wait_ge(t1c, n + 1)
                            pe.wait_ge(m2c, n + 1)
                            for k in range(KD):
                                mm(X1[:, :], xsT[:, k, :], e_w1[:, k, bass.ds(e * HE, HE)], start=(k == 0), stop=False)
                            mm(X1[:, :], ones3[:, :], bias3[:, bass.ds(e * HE, HE)], start=False, stop=True).then_inc(m1, 1)
                            pe.wait_ge(m1c, n + 1)
                            for k in range(HE // P):
                                ins = nc.tensor.transpose(X0[:, k * P:(k + 1) * P], hs[:, k * P:(k + 1) * P], ident[:, :])
                            ins.then_inc(t2, 1)
                            pe.wait_ge(t2c, n + 2)
                            for k in range(HE // P):
                                mm(X1[:, 0:D], hT[:, k, :], e_w2[:, k, bass.ds(e * D, D)], start=(k == 0), stop=False)
                            mm(X1[:, 0:D], ones3[:, :], bias3[:, bass.ds(e * D + E * HE, D)], start=False, stop=True).then_inc(m2, 1)


def blocks(nc, g):
    for name, shape in (("x1_s", [B, L, D]), ("xn1_s", [B, L, D]), ("xn1T_s", [B, P, KD, L]), ("m_s", [B, L, D]),
                        ("xs_s", [S, D]), ("y0_s", [S, D]), ("y1_s", [S, D]), ("part_s", [NT // 4, 4 * P, D])):
        g[name] = nc.dram_tensor(name, shape, F32).ap()
    with nc.sbuf_tensor("lg", [P, NT, E], F32) as lg:
        g["lg"] = lg
        phase_a(nc, g)
        phase_m(nc, g)
        phase_e(nc, g)


INPUTS = (
    [(n, "L0_attn_" + n, False) for n in ("bq", "bk", "ln1_g", "ln1_b", "ln2_g", "ln2_b", "b1", "bv", "bo", "b2",
                                          "wq", "wk", "wv", "wo", "w1", "w2", "x")]
    + [("proj", "L0_attn_proj_mat", False), ("mu_r", "L0_ffn_mu_r", False), ("mu_k", "L0_ffn_mu_k", False)]
    + [(f"W_{n}T", "L0_ffn_W_" + n, True) for n in "rkv"]
    + [(n + "T", "L1_attn_" + n, True) for n in ("W_in", "W_xproj", "W_dt", "W_out")]
    + [(n, "L1_attn_" + n, False) for n in ("A_log", "conv_w", "conv_b", "b_dt", "D_skip")]
    + [(n, "L1_ffn_" + n, False) for n in ("gate_W", "gate_b", "ln_gamma", "ln_beta")]
    + [("e_" + n, "L1_ffn_" + n, False) for n in ("W1", "b1", "W2", "b2")]
)


def kernel(**inputs):
    import concourse.bacc as bacc
    from concourse.bass_utils import run_bass_kernel_spmd

    nc = bacc.Bacc("TRN2", target_bir_lowering=False, num_devices=1)
    arrays, g = {}, {}
    for name, source, transposed in INPUTS:
        a = np.asarray(inputs[source])
        arrays["in_" + name] = np.ascontiguousarray(a.T if transposed else a)
    arrays["in_ident"] = np.eye(P, dtype=np.float32)
    for name, a in arrays.items():
        g[name[3:]] = nc.dram_tensor(name, a.shape, F32, kind="ExternalInput").ap()
    g["out"] = nc.dram_tensor("out", [B, L, D], F32, kind="ExternalOutput").ap()
    blocks(nc, g)
    r = run_bass_kernel_spmd(nc, [arrays], core_ids=[0])
    return r.results[0]["out"]
```

```python
import numpy as np
from contextlib import ExitStack
import concourse.bass as bass
from concourse import mybir

F32 = mybir.dt.float32
BF16 = mybir.dt.bfloat16
I32 = mybir.dt.int32
ALU = mybir.AluOpType
ACT = mybir.ActivationFunctionType
AX = mybir.AxisListType

B, L, D = 4, 1024, 256
P = 128
TB = L // P
NT = B * TB
KD = D // P
CH = 512
NC_ = L // CH
EPS = 1e-5

H, DH, M = 16, 16, 128
FF = 1024
MF = FF // P
ROUND = 1.5 * 2.0 ** 23
TURN = float(np.nextafter(np.float32(2 * np.pi), np.float32(0)))
RSQRT_SEED = float(0x5F3759DF)

E, HE = 8, 512


class Ring:

    def __init__(self, names, n):
        self.n = n
        self.of = {}
        self.uses = [0] * n
        for i, name in enumerate(names):
            s = i % n
            self.of[name] = (s, self.uses[s])
            self.uses[s] += 1


JOBS_A = (
    [("xt", c) for c in range(NC_)] + [("x2", c) for c in range(NC_)]
    + [("q", m) for m in range(KD)] + [("k", m) for m in range(KD)] + [("v", i) for i in range(2)]
    + [("kf", n) for n in range(16)] + [("qf", n) for n in range(16)]
    + [("wo", i) for i in range(2)] + [("r", i) for i in range(2)] + [("kk", m) for m in range(KD)] + [("xf", c) for c in range(NC_)]
    + [j for c in range(NC_) for j in [("h", c, q) for q in range(MF // 2)] + [("w2", c)]]
    + [("vv", i) for i in range(2)]
    + [("xn", c) for c in range(NC_)] + [("gate",)]
)


def phase_a(nc, g):
    ring = Ring(JOBS_A, 3)
    ctx = ExitStack()
    with ctx:
        def sb(name, shape, dt=F32):
            return ctx.enter_context(nc.sbuf_tensor(name, shape, dt))

        def sem(name):
            return ctx.enter_context(nc.semaphore(name))

        wq, wk, wv, wo = (sb(n, [P, KD, D]) for n in ("wq", "wk", "wv", "wo"))
        wr, wkk, wvv = (sb(n, [P, KD, D]) for n in ("wr", "wkk", "wvv"))
        w1 = sb("w1", [P, KD, FF])
        w2 = sb("w2", [P, MF, D])
        gate_w = sb("gate_w", [P, KD, E])
        proj = sb("proj", [P, 2, M])
        cols = sb("cols", [P, 8, KD])
        b1c = sb("b1c", [P, MF])
        omu = sb("omu", [P, 2, KD])
        ident = sb("ident_a", [P, P])
        halfpi = sb("halfpi", [P, 1])
        rnd = sb("rnd", [P, 1])
        brow = sb("brow", [1, 3 * D + E])
        bsp = sb("bsp", [1, 3, 3 * D + E], BF16)
        brs = sb("brs", [1, 3 * D + E])
        bias3 = sb("bias3", [3, 3 * D + E], BF16)
        ones3 = sb("ones3", [3, P], BF16)

        xin = sb("xin", [P, TB, D])
        xres = sb("xres", [P, TB, D])
        xn = sb("xn_a", [P, TB, D])
        xh = sb("xh", [P, TB, D])
        s1 = sb("s1", [P, TB, D])
        st = sb("st_a", [P, TB, 6])
        mv = sb("mv_a", [P, TB, 2])
        rs = sb("rs_a", [P, 4, TB])
        spare = sb("spare_a", [P, 1])
        xnT = sb("xnT_a", [P, KD, 1 + L])
        x2T = sb("x2T", [P, KD, L])
        qkh = sb("qkh", [P, MF, CH])
        qT = qkh[:, 0:4, :].rearrange("p (m c) t -> p m (c t)", m=KD)
        kT = qkh[:, 4:8, :].rearrange("p (m c) t -> p m (c t)", m=KD)
        v = sb("v", [P, TB, D])
        turns = sb("turns", [P, 2 * CH])
        rr = sb("rr", [P, 2, 2 * CH])
        ra = sb("ra", [P, 2, 2 * CH])
        fs = sb("fs", [P, 2, 2 * CH])
        fc = sb("fc", [P, 2, 2 * CH])
        kvs = sb("kvs", [P, 2 * M])
        kv = sb("kv", [P, H // 2, 2, 2, 2 * DH])
        aT = sb("aT", [P, KD, L])
        xr = sb("xr", [P, KD, L])
        xk = sb("xk", [P, KD, L])
        kr = sb("kr", [P, KD, L])

        W = [ctx.enter_context(nc.psum_tensor(f"work{i}", [P, 2 * CH], F32)) for i in range(3)]
        kvp = ctx.enter_context(nc.psum_tensor("kvp", [P, CH], F32))
        atp = ctx.enter_context(nc.psum_tensor("atp", [P, CH], F32))
        sums = (kvp, atp)

        w_in = sem("w_in"); bias_in = sem("bias_in"); bias_split = sem("bias_split")
        zeroed = sem("zeroed"); prep = sem("prep")
        xin_in = sem("xin_in"); xres_in = sem("xres_in"); stored = sem("stored")
        full = [sem(f"full{i}") for i in range(3)]
        dve = sem("dve_chain")
        xn_ok = sem("xn_ok"); x2_ok = sem("x2_ok"); xh_ok = sem("xh_ok"); s1_ok = sem("s1_ok")
        tr_ok = sem("tr_ok"); qk_ok = sem("qk_ok"); v_ok = sem("v_ok")
        turns_ok = sem("turns_ok"); rr_ok = sem("rr_ok"); ra_ok = sem("ra_ok")
        feat_ok = sem("feat_ok"); feat_used = sem("feat_used")
        kv_ok = sem("kv_ok"); kvs_ok = sem("kvs_ok"); kv_turned = sem("kv_turned"); at_ok = sem("at_ok")
        h_ok = sem("h_ok"); mix_ok = sem("mix_ok"); th_ok = sem("th_ok")
        kr_ok = sem("kr_ok"); kact_ok = sem("kact_ok"); out_ok = sem("out_ok"); g_ok = sem("g_ok")
        x1_ok = sem("x1_ok"); xnT_ok = sem("xnT_ok"); lg_ok = sem("lg_ok")

        READ = {}
        for c in range(NC_):
            READ["xt", c] = (tr_ok, 6, c + 1)
            READ["x2", c] = (tr_ok, 6, c + 3)
            READ["xf", c] = (tr_ok, 6, c + 5)
            READ["w2", c] = (s1_ok, 4, c + 3)
            READ["xn", c] = (xnT_ok, 2, c + 1)
            for q in range(MF // 2):
                READ["h", c, q] = (h_ok, MF, c * MF // 2 + q + 1)
        for m in range(KD):
            READ["q", m] = (qk_ok, 4, m + 1)
            READ["k", m] = (qk_ok, 4, m + 3)
            READ["kk", m] = (kr_ok, 2, m + 1)
        for i in range(2):
            READ["v", i] = (v_ok, 2, i + 1)
            READ["wo", i] = (s1_ok, 4, i + 1)
            READ["r", i] = (th_ok, 2, i + 1)
            READ["vv", i] = (out_ok, 2, i + 1)
        for n in range(16):
            READ["kf", n] = (rr_ok, 32, n + 1)
            READ["qf", n] = (rr_ok, 32, n + 17)
        READ["gate",] = (lg_ok, 1, 1)

        def slot(*job):
            return W[ring.of[job][0]]

        def wait_full(e, b, *job):
            s, use = ring.of[job]
            e.wait_ge(full[s], b * ring.uses[s] + use + 1)

        def wait_slot(e, b, *job):
            at = JOBS_A.index(job)
            if at >= 3:
                s, per, k = READ[JOBS_A[at - 3]]
                e.wait_ge(s, b * per + k)

        with nc.Block() as block:
            @block.sync
            def _(sp):
                def load(dst, src):
                    sp.dma_start(dst, src).then_inc(w_in, 16)

                tokens = lambda ap: ap.rearrange("(t p) d -> p t d", p=P)
                sp.dma_start(xin[:, :, :], tokens(g["x"][0])).then_inc(xin_in, 16)
                load(ident[:, :], g["ident"])
                with nc.allow_non_contiguous_dma(reason="vectors by channel, once"):
                    for i, n in enumerate(("bq", "bk", "ln1_g", "ln1_b", "ln2_g", "ln2_b", "mu_r", "mu_k")):
                        load(cols[:, i, :], g[n].rearrange("(k p) -> p k", p=P))
                    load(b1c[:, :], g["b1"].rearrange("(k p) -> p k", p=P))
                for i, n in enumerate(("bv", "bo", "b2", "gate_b")):
                    load(brow[:, i * D:i * D + g[n].shape[0]], g[n].rearrange("(a n) -> a n", a=1))
                for t, n in ((wq, "wq"), (wk, "wk"), (wv, "wv"), (wo, "wo"), (wr, "W_rT"), (wkk, "W_kT"), (wvv, "W_vT"),
                             (w1, "w1"), (w2, "w2"), (gate_w, "gate_W")):
                    load(t[:, :, :], g[n].rearrange("(k p) n -> p k n", p=P))
                sp.wait_ge(zeroed, 1)
                for r in range(4):
                    for e in range(2):
                        load(proj[32 * r + 16 * e:32 * r + 16 * e + 16, e, :], g["proj"])
                sp.wait_ge(bias_split, 6)
                for i in range(3):
                    sp.dma_start(bias3[i:i + 1, :], bsp[:, i, :]).then_inc(bias_in, 16)

                def batch(b, last):
                    sp.dma_start(xres[:, :, :], tokens(g["x"][b])).then_inc(xres_in, 16)
                    if not last:
                        sp.wait_ge(tr_ok, b * 6 + 4)
                        sp.dma_start(xin[:, :, :], tokens(g["x"][b + 1])).then_inc(xin_in, 16)
                    sp.wait_ge(x1_ok, b + 1)
                    sp.dma_start(tokens(g["x1_s"][b]), s1[:, :, :]).then_inc(stored, 16)
                    sp.wait_ge(xh_ok, b * 2 * TB + 2 * TB)
                    sp.dma_start(tokens(g["xn1_s"][b]), xh[:, :, :]).then_inc(stored, 16)
                    sp.wait_ge(xnT_ok, b * NC_ + NC_)
                    sp.dma_start(g["xn1T_s"][b], kr[:, :, :]).then_inc(stored, 16)

                with sp.Fori(0, B - 1) as b:
                    batch(b, False)
                batch(B - 1, True)
                sp.wait_ge(stored, 48 * B)

            @block.gpsimd
            def _(pool):
                nc.gpsimd.memset(proj[:, :, :], 0.0).then_inc(zeroed, 1)
                nc.gpsimd.memset(halfpi[:, :], float(np.float32(np.pi / 2))).then_inc(prep, 1)
                nc.gpsimd.memset(rnd[:, :], ROUND).then_inc(prep, 1)
                nc.gpsimd.memset(ones3[:, :], 1.0).then_inc(prep, 1)
                nc.gpsimd.memset(kv[:, :, :, :, :], 0.0).then_inc(prep, 1)
                nc.gpsimd.memset(xnT[:, :, 0:1], 0.0).then_inc(prep, 1)
                with pool.Fori(0, B) as b:
                    for m in range(KD):
                        pool.wait_ge(kr_ok, b * KD + m + 1)
                        nc.gpsimd.tensor_tensor(aT[:, m, :], kr[:, m, :], kr[:, m, :], ALU.mult).then_inc(kact_ok, 1)

            LN_LINKS = 2 * TB + 1 + 3 + 16
            DVE_LINKS = 4 * LN_LINKS + 2 * KD + 2

            def layer_norm_stats(v_, link, src, ready=None):
                for t in range(TB):
                    if ready:
                        ready(t)
                    v_.bn_stats(st[:, t, :], src[:, t, :]).then_inc(dve, 1)
                link(TB)
                v_.memset(spare[:, :], 0.0).then_inc(dve, 1)
                for t in range(TB):
                    v_.bn_aggr(mv[:, t, :], st[:, t, :]).then_inc(dve, 1)
                link(TB + 1)
                var, y, y2, h = (rs[:, i, :] for i in range(4))
                v_.tensor_scalar(var, mv[:, :, 1], EPS, None, ALU.add).then_inc(dve, 1)
                link(1)
                v_.tensor_scalar(h.bitcast(I32), var.bitcast(I32), 1, None, ALU.logical_shift_right).then_inc(dve, 1)
                link(1)
                v_.tensor_scalar(y.bitcast(I32), h.bitcast(I32), -1.0, RSQRT_SEED, ALU.mult, ALU.add).then_inc(dve, 1)
                link(1)
                for _ in range(4):
                    v_.tensor_tensor(y2, y, y, ALU.mult).then_inc(dve, 1)
                    link(1)
                    v_.tensor_tensor(y2, y2, var, ALU.mult).then_inc(dve, 1)
                    link(1)
                    v_.tensor_scalar(y2, y2, -0.5, 1.5, ALU.mult, ALU.add).then_inc(dve, 1)
                    link(1)
                    v_.tensor_tensor(y, y, y2, ALU.mult).then_inc(dve, 1)
                    link(1)

            def normalise(v_, dst, src, ok):
                for t in range(TB):
                    v_.tensor_scalar(dst[:, t, :], src[:, t, :], mv[:, t, 0:1], rs[:, 1, t:t + 1],
                                     ALU.subtract, ALU.mult).then_inc(ok, 1)

            @block.vector
            def _(dv):
                v_ = nc.vector
                dv.wait_ge(w_in, 16 * (1 + 9 + 4 + 10 + 8))
                src = brow
                for i in range(3):
                    v_.tensor_copy(bsp[:, i, :], src[:, :]).then_inc(bias_split, 1)
                    dv.wait_ge(bias_split, 2 * i + 1)
                    v_.tensor_tensor(brs[:, :], src[:, :], bsp[:, i, :], ALU.subtract).then_inc(bias_split, 1)
                    dv.wait_ge(bias_split, 2 * i + 2)
                    src = brs
                v_.tensor_scalar(omu[:, :, :], cols[:, 6:8, :], -1.0, 1.0, ALU.mult, ALU.add).then_inc(prep, 1)
                v_.tensor_scalar(proj[:, :, :], proj[:, :, :], float(np.float32(1 / (8 * np.pi))), None, ALU.mult).then_inc(prep, 1)
                dv.wait_ge(prep, 7)

                def evac_attention(b, q):
                    dv.wait_ge(feat_used, b * 32 + 16 + 4 * q + 4)
                    v_.tensor_copy(aT[:, q // 2, (q % 2) * CH:(q % 2 + 1) * CH], atp[:, :]).then_inc(at_ok, 1)

                four = lambda ap, i: ap[:, 4 * i:4 * i + 4, :].rearrange("p t d -> p (t d)")
                def input_norms(b, link):
                    dv.wait_ge(xin_in, b * 16 + 16)
                    layer_norm_stats(v_, link, xin)
                    normalise(v_, xn, xin, xn_ok)
                    layer_norm_stats(v_, link, xn, lambda t: dv.wait_ge(xn_ok, b * TB + t + 1))
                    normalise(v_, xin, xn, x2_ok)

                def batch(b, last):
                    n = [2 * LN_LINKS]

                    def link(k):
                        n[0] += k
                        dv.wait_ge(dve, b * DVE_LINKS + n[0])

                    dv.wait_ge(tr_ok, b * 6 + 2)
                    for i, dst in enumerate((xr, xk)):
                        for k in range(KD):
                            v_.tensor_scalar(dst[:, k, :], xnT[:, k, 0:L], omu[:, i, k:k + 1], None, ALU.mult).then_inc(dve, 1)
                    link(2 * KD)
                    for i, dst in enumerate((xr, xk)):
                        for k in range(KD):
                            v_.scalar_tensor_tensor(dst[:, k, :], xnT[:, k, 1:L + 1], cols[:, 6 + i, k:k + 1], dst[:, k, :],
                                                    ALU.mult, ALU.add).then_inc(mix_ok, 1)
                    for i in range(2):
                        wait_full(dv, b, "v", i)
                        v_.tensor_copy(four(v, i), slot("v", i)[:, :]).then_inc(v_ok, 1)
                    for s in range(32):
                        job = ("kf", s) if s < 16 else ("qf", s - 16)
                        if s % 4 == 2 and 6 <= s <= 18:
                            g_ = (s - 6) // 4
                            bank = sums[g_ % 2]
                            dv.wait_ge(feat_used, b * 32 + 4 * g_ + 4)
                            v_.tensor_copy(kvs[:, :], bank[:, 0:2 * M]).then_inc(kvs_ok, 1)
                            dv.wait_ge(kv_turned, b * 4 + g_ + 1)
                            for e in range(2):
                                turned = bank[:, (2 + e) * M:(3 + e) * M].rearrange("p (i c d) -> p i c d", i=2, c=2)
                                v_.tensor_scalar(kv[:, 2 * g_:2 * g_ + 2, e, :, DH * e:DH * e + DH], turned[:, :, :, DH * e:DH * e + DH],
                                                 1.0 / M, None, ALU.mult).then_inc(kv_ok, 1)
                        dv.wait_ge(turns_ok, b * 32 + s + 1)
                        if s >= 2:
                            dv.wait_ge(feat_ok, b * 64 + 2 * (s - 1))
                        v_.scalar_tensor_tensor(rr[:, s % 2, :], turns[:, :], ROUND, slot(*job)[:, :],
                                                ALU.subtract, ALU.subtract).then_inc(rr_ok, 1)
                        dv.wait_ge(rr_ok, b * 32 + s + 1)
                        v_.tensor_scalar(ra[:, s % 2, :].bitcast(I32), rr[:, s % 2, :].bitcast(I32), 0x7FFFFFFF, None, ALU.bitwise_and).then_inc(ra_ok, 1)
                        if s >= 21 and s % 4 == 1:
                            evac_attention(b, (s - 21) // 4)
                    evac_attention(b, 3)
                    for i in range(2):
                        wait_full(dv, b, "wo", i)
                        v_.tensor_tensor(four(s1, i), slot("wo", i)[:, :], four(xn, i), ALU.add).then_inc(s1_ok, 1)
                    dv.wait_ge(s1_ok, b * 4 + 2)
                    layer_norm_stats(v_, link, s1)
                    normalise(v_, xh, s1, xh_ok)
                    if not last:
                        dv.wait_ge(xh_ok, b * 2 * TB + TB)
                        input_norms(b + 1, link)
                        dv.wait_ge(x2_ok, b * TB + 2 * TB)
                    for c in range(NC_):
                        wait_full(dv, b, "w2", c)
                        v_.tensor_tensor(four(s1, c), slot("w2", c)[:, :], four(s1, c), ALU.add).then_inc(s1_ok, 1)
                    for i in range(2):
                        wait_full(dv, b, "vv", i)
                        dv.wait_ge(th_ok, b * 2 + i + 1)
                        v_.scalar_tensor_tensor(four(v, i), four(v, i), 1.0, slot("vv", i)[:, :], ALU.add, ALU.mult).then_inc(out_ok, 1)
                    dv.wait_ge(s1_ok, b * 4 + 4)
                    for i in range(2):
                        dv.wait_ge(g_ok, b * 2 + i + 1)
                        v_.tensor_tensor(four(s1, i), four(s1, i), four(v, i), ALU.mult).then_inc(dve, 1)
                    link(2)
                    dv.wait_ge(xres_in, b * 16 + 16)
                    v_.tensor_tensor(s1[:, :, :], s1[:, :, :], xres[:, :, :], ALU.add).then_inc(x1_ok, 1)
                    dv.wait_ge(x1_ok, b + 1)
                    layer_norm_stats(v_, link, s1)
                    normalise(v_, xh, s1, xh_ok)
                    wait_full(dv, b, "gate")
                    v_.tensor_copy(g["lg"][:, bass.ds(b * TB, TB), :],
                                   slot("gate")[:, 0:TB * E].rearrange("p (t e) -> p t e", t=TB)).then_inc(lg_ok, 1)
                    dv.wait_ge(stored, b * 48 + 48)
                    assert n[0] == (DVE_LINKS if last else DVE_LINKS + 2 * LN_LINKS)

                chained = [0]

                def first_link(k):
                    chained[0] += k
                    dv.wait_ge(dve, chained[0])

                input_norms(0, first_link)
                with dv.Fori(0, B - 1) as b:
                    batch(b, False)
                batch(B - 1, True)

            @block.scalar
            def _(ac):
                A = nc.scalar.activation

                def copy_transposed(b, name, c, dst, ok, **scale):
                    wait_full(ac, b, name, c)
                    for k in range(KD):
                        i = A(dst(k), slot(name, c)[:, k * CH:(k + 1) * CH], ACT.Identity, **{n: f(k) for n, f in scale.items()})
                    i.then_inc(ok, 1)

                ac.wait_ge(w_in, 16 * (1 + 9 + 4 + 10 + 8))
                ac.wait_ge(prep, 7)
                with ac.Fori(0, B) as b:
                    for c in range(NC_):
                        copy_transposed(b, "xt", c, lambda k: xnT[:, k, 1 + c * CH:1 + (c + 1) * CH], tr_ok)
                    for c in range(NC_):
                        copy_transposed(b, "x2", c, lambda k: x2T[:, k, c * CH:(c + 1) * CH], tr_ok,
                                        scale=lambda k: cols[:, 2, k:k + 1], bias=lambda k: cols[:, 3, k:k + 1])
                    for i, (name, dst) in enumerate((("q", qT), ("k", kT))):
                        for m in range(KD):
                            wait_full(ac, b, name, m)
                            A(dst[:, m, :], slot(name, m)[:, :], ACT.Identity, bias=cols[:, i, m:m + 1]).then_inc(qk_ok, 1)

                    def whole_turns(s):
                        job = ("kf", s) if s < 16 else ("qf", s - 16)
                        wait_full(ac, b, *job)
                        if s:
                            ac.wait_ge(rr_ok, b * 32 + s)
                        A(turns[:, :], slot(*job)[:, :], ACT.Identity, bias=rnd[:, :]).then_inc(turns_ok, 1)

                    whole_turns(0)
                    for s in range(32):
                        if s < 31:
                            whole_turns(s + 1)
                        ac.wait_ge(rr_ok, b * 32 + s + 1)
                        if s >= 2:
                            ac.wait_ge(feat_used, b * 32 + s - 1)
                        A(fs[:, s % 2, :], rr[:, s % 2, :], ACT.Sin, scale=-TURN).then_inc(feat_ok, 1)
                        ac.wait_ge(ra_ok, b * 32 + s + 1)
                        A(fc[:, s % 2, :], ra[:, s % 2, :], ACT.Sin, scale=-TURN, bias=halfpi[:, :]).then_inc(feat_ok, 1)
                    for i in range(2):
                        wait_full(ac, b, "r", i)
                        A(v[:, 4 * i:4 * i + 4, :].rearrange("p t d -> p (t d)"), slot("r", i)[:, :], ACT.Tanh, scale=0.5).then_inc(th_ok, 1)
                    for m in range(KD):
                        wait_full(ac, b, "kk", m)
                        A(kr[:, m, :], slot("kk", m)[:, :], ACT.Relu).then_inc(kr_ok, 1)
                    for c in range(NC_):
                        copy_transposed(b, "xf", c, lambda k: x2T[:, k, c * CH:(c + 1) * CH], tr_ok,
                                        scale=lambda k: cols[:, 4, k:k + 1], bias=lambda k: cols[:, 5, k:k + 1])
                    for c in range(NC_):
                        for q in range(MF // 2):
                            wait_full(ac, b, "h", c, q)
                            if c and not q:
                                wait_full(ac, b, "w2", c - 1)
                            for j in range(2):
                                i = A(qkh[:, 2 * q + j, :], slot("h", c, q)[:, j * CH:(j + 1) * CH], ACT.Relu,
                                      bias=b1c[:, 2 * q + j:2 * q + j + 1])
                            i.then_inc(h_ok, 1)
                    for i in range(2):
                        ac.wait_ge(out_ok, b * 2 + i + 1)
                        A(v[:, 4 * i:4 * i + 4, :], v[:, 4 * i:4 * i + 4, :], ACT.Silu, scale=0.5).then_inc(g_ok, 1)
                    for c in range(NC_):
                        copy_transposed(b, "xn", c, lambda k: kr[:, k, c * CH:(c + 1) * CH], xnT_ok)

            @block.tensor
            def _(pe):
                mm = nc.tensor.matmul
                pe.wait_ge(w_in, 16 * (1 + 9 + 4 + 10 + 8))
                pe.wait_ge(prep, 7)
                pe.wait_ge(bias_in, 48)

                def done(ins, *job):
                    ins.then_inc(full[ring.of[job][0]], 1)

                def transposes(b, name, c, src):
                    wait_slot(pe, b, name, c)
                    for k in range(KD):
                        for t in range(4):
                            i = nc.tensor.transpose(slot(name, c)[:, k * CH + t * P:k * CH + (t + 1) * P],
                                                    src[:, 4 * c + t, k * P:(k + 1) * P], ident[:, :])
                    done(i, name, c)

                def by_channel(b, job, w, x, m):
                    wait_slot(pe, b, *job)
                    for c in range(NC_):
                        for k in range(KD):
                            i = mm(slot(*job)[:, c * CH:(c + 1) * CH], w[:, k, m * P:(m + 1) * P], x[:, k, c * CH:(c + 1) * CH],
                                   start=(k == 0), stop=(k == KD - 1))
                    done(i, *job)

                def by_token(b, job, x, w, bias, nk=KD):
                    wait_slot(pe, b, *job)
                    for t in range(4):
                        out = slot(*job)[:, t * D:(t + 1) * D]
                        for k in range(nk):
                            i = mm(out, x(k, t), w[:, k, :], start=(k == 0), stop=(k == nk - 1 and bias is None))
                        if bias is not None:
                            i = mm(out, ones3[:, :], bias3[:, bias * D:(bias + 1) * D], start=False, stop=True)
                    done(i, *job)

                with pe.Fori(0, B) as b:
                    for c in range(NC_):
                        pe.wait_ge(xn_ok, b * TB + 4 * c + 4)
                        transposes(b, "xt", c, xn)
                    for c in range(NC_):
                        pe.wait_ge(x2_ok, b * TB + 4 * c + 4)
                        transposes(b, "x2", c, xin)
                    pe.wait_ge(tr_ok, b * 6 + 4)
                    for m in range(KD):
                        by_channel(b, ("q", m), wq, x2T, m)
                    for m in range(KD):
                        by_channel(b, ("k", m), wk, x2T, m)
                    for i in range(2):
                        by_token(b, ("v", i), lambda k, t: x2T[:, k, (4 * i + t) * P:(4 * i + t + 1) * P], wv, 0)

                    def key_turns(s):
                        mt, j, tp = s // 8, s // 4 % 2, s % 4
                        wait_slot(pe, b, "kf", s)
                        if s == 0:
                            pe.wait_ge(qk_ok, b * 4 + 4)
                        for tt in range(2):
                            for i in range(2):
                                r = 32 * (2 * j + i)
                                t = 2 * tp + tt
                                ins = mm(slot("kf", s)[:, i * CH + tt * 2 * M:i * CH + (tt + 1) * 2 * M],
                                         kT[r:r + 32, mt, t * P:(t + 1) * P], proj[r:r + 32, :, :].rearrange("p e m -> p (e m)"),
                                         start=True, stop=True)
                        done(ins, "kf", s)

                    def query_turns(s):
                        mt, c, j, e = s // 8, s // 4 % 2, s // 2 % 2, s % 2
                        wait_slot(pe, b, "qf", s)
                        for i in range(2):
                            r = 32 * (2 * j + i)
                            ins = mm(slot("qf", s)[:, i * CH:(i + 1) * CH], proj[r:r + 32, e, :], qT[r:r + 32, mt, c * CH:(c + 1) * CH],
                                     start=True, stop=True)
                        done(ins, "qf", s)

                    def key_sums(s):
                        mt, j, tp = s // 8, s // 4 % 2, s % 4
                        pe.wait_ge(feat_ok, b * 64 + 2 * s + 2)
                        if s == 0:
                            pe.wait_ge(v_ok, b * 2 + 2)
                        g_ = s // 4
                        if tp == 0 and g_ >= 2:
                            pe.wait_ge(kv_ok, b * 8 + 2 * g_ - 2)
                        for tt in range(2):
                            for i in range(2):
                                for cs, f in enumerate((fs, fc)):
                                    pair = mt * 4 + 2 * j + i
                                    r = 32 * (2 * i + cs)
                                    ins = mm(sums[g_ % 2][r:r + 32, 0:2 * M], v[:, 2 * tp + tt, pair * 2 * DH:(pair + 1) * 2 * DH],
                                             f[:, s % 2, i * CH + tt * 2 * M:i * CH + (tt + 1) * 2 * M],
                                             start=(tp == 0 and tt == 0), stop=(tp == 3 and tt == 1))
                        ins.then_inc(feat_used, 1)

                    def turn_sums(g_):
                        pe.wait_ge(kvs_ok, b * 4 + g_ + 1)
                        for e in range(2):
                            ins = nc.tensor.transpose(sums[g_ % 2][:, (2 + e) * M:(3 + e) * M], kvs[:, e * M:(e + 1) * M], ident[:, :])
                        ins.then_inc(kv_turned, 1)

                    def attend(s):
                        mt, c, j, e = s // 8, s // 4 % 2, s // 2 % 2, s % 2
                        q = s // 4
                        pe.wait_ge(feat_ok, b * 64 + 32 + 2 * s + 2)
                        if s == 0:
                            pe.wait_ge(kv_ok, b * 8 + 8)
                        if s % 4 == 0 and q:
                            pe.wait_ge(at_ok, b * 4 + q)
                        for cs, f in enumerate((fs, fc)):
                            for i in range(2):
                                a = 2 * j + i
                                ins = mm(atp[32 * a:32 * a + 32, :], kv[:, mt * 4 + a, e, cs, :], f[:, s % 2, i * CH:(i + 1) * CH],
                                         start=(e == 0 and cs == 0), stop=(e == 1 and cs == 1))
                        return ins

                    for s in range(32 + 2):
                        if s < 32:
                            key_turns(s) if s < 16 else query_turns(s - 16)
                        u = s - 2
                        if 0 <= u < 16:
                            key_sums(u)
                        if s % 4 == 2 and 6 <= s <= 18:
                            turn_sums((s - 6) // 4)
                        if u >= 16:
                            attend(u - 16).then_inc(feat_used, 1)
                    pe.wait_ge(at_ok, b * 4 + 4)
                    for i in range(2):
                        by_token(b, ("wo", i), lambda k, t: aT[:, k, (4 * i + t) * P:(4 * i + t + 1) * P], wo, 1)
                    pe.wait_ge(mix_ok, b * 4 + 4)
                    for i in range(2):
                        by_token(b, ("r", i), lambda k, t: xr[:, k, (4 * i + t) * P:(4 * i + t + 1) * P], wr, None)
                    for m in range(KD):
                        by_channel(b, ("kk", m), wkk, xk, m)
                    for c in range(NC_):
                        pe.wait_ge(xh_ok, b * 2 * TB + 4 * c + 4)
                        transposes(b, "xf", c, xh)
                    for c in range(NC_):
                        pe.wait_ge(tr_ok, b * 6 + 5 + c)
                        for q in range(MF // 2):
                            wait_slot(pe, b, "h", c, q)
                            for j in range(2):
                                m = 2 * q + j
                                for k in range(KD):
                                    ins = mm(slot("h", c, q)[:, j * CH:(j + 1) * CH], w1[:, k, m * P:(m + 1) * P],
                                             x2T[:, k, c * CH:(c + 1) * CH], start=(k == 0), stop=(k == KD - 1))
                            done(ins, "h", c, q)
                        pe.wait_ge(h_ok, b * MF + (c + 1) * MF // 2)
                        by_token(b, ("w2", c), lambda k, t: qkh[:, k, t * P:(t + 1) * P], w2, 2, MF)
                    pe.wait_ge(kact_ok, b * KD + KD)
                    for i in range(2):
                        by_token(b, ("vv", i), lambda k, t: aT[:, k, (4 * i + t) * P:(4 * i + t + 1) * P], wvv, None)
                    for c in range(NC_):
                        pe.wait_ge(xh_ok, b * 2 * TB + TB + 4 * c + 4)
                        transposes(b, "xn", c, xh)
                    wait_slot(pe, b, "gate")
                    pe.wait_ge(xnT_ok, b * 2 + 2)
                    for t in range(TB):
                        out = slot("gate")[:, t * E:(t + 1) * E]
                        for k in range(KD):
                            mm(out, kr[:, k, t * P:(t + 1) * P], gate_w[:, k, :], start=(k == 0), stop=False)
                        ins = mm(out, ones3[:, :], bias3[:, 3 * D:3 * D + E], start=False, stop=True)
                    done(ins, "gate")
                    pe.wait_ge(lg_ok, b + 1)


DI, NS, DC, DR = 512, 16, 4, 16
KI = DI // P
NO = NS // 2
JOBS_M = [("in", j) for j in range(2 * KI)] + [("bc",)] + [("dt", m) for m in range(KI)]


def phase_m(nc, g):
    ring = Ring(JOBS_M, 3)
    with ExitStack() as ctx:
        def sb(name, shape, dt=F32):
            return ctx.enter_context(nc.sbuf_tensor(name, shape, dt))

        def sem(name):
            return ctx.enter_context(nc.semaphore(name))

        w_in = sb("mw_in", [P, KD, 2 * DI])
        w_bc = sb("mw_bc", [P, KI, 6 * NS + DR])
        w_dt = sb("mw_dt", [DR, DI])
        w_out = sb("mw_out", [P, KI, D])
        acol = sb("acol", [P, KI, NS])
        taps = sb("taps", [P, KI, DC])
        vecs = sb("vecs", [P, 3, KI])
        one = sb("one", [P, 1])
        pick = sb("pick", [3 * 2 * NS, 2 * NS, P], BF16)
        ident = sb("ident_m", [P, P])

        xT = sb("m_xT", [P, KD, L])
        xi = sb("m_xi", [P, KI, DC - 1 + L])
        zs = sb("m_zs", [P, KI * L])
        u = sb("m_u", [P, KI * L])
        dt = sb("m_dt", [P, KI * L])
        du = sb("m_du", [P, KI * L])
        bcs = sb("m_bcs", [3 * 2 * NS, L], BF16)
        bc2 = sb("m_bc2", [3 * 2 * NS, L], BF16)
        bcr = sb("m_bcr", [3 * 2 * NS, L])
        dr = sb("m_dr", [DR, L])
        c_even = sb("m_c_even", [P, L])
        c_odd = sb("m_c_odd", [P, L])
        dA = sb("m_dA", [P, 2, L])
        dB = sb("m_dB", [P, 2, L])
        soft = (dA, dB)
        csb = (c_even, c_odd)
        h = sb("m_h", [P, 2, L])
        pr = sb("m_pr", [P, 2, L])
        yT = sb("m_yT", [P, KI * L])
        so = sb("m_so", [P, TB, D])

        W = [ctx.enter_context(nc.psum_tensor(f"m_work{i}", [P, 2 * CH], F32)) for i in range(3)]
        X = W[2]
        b_slot = lambda s: W[2 * s % 3]
        c_slot = lambda s: W[(2 * s + 1) % 3]
        Y = ctx.enter_context(nc.psum_tensor("m_Y", [P, 2 * CH], F32))

        w_ok = sem("m_w_in"); prep = sem("m_prep"); x_in = sem("m_x_in"); stored = sem("m_stored")
        full = [sem(f"m_full{i}") for i in range(3)]
        xi_ok = sem("m_xi_ok"); z_ok = sem("m_z_ok"); chain = sem("m_chain"); conv_ok = sem("m_conv_ok"); u_ok = sem("m_u_ok")
        dr_ok = sem("m_dr_ok"); bcs_ok = sem("m_bcs_ok"); bc_split = sem("m_bc_split"); soft_ok = sem("m_soft"); log_ok = sem("m_log")
        dt_ok = sem("m_dt_ok"); du_ok = sem("m_du_ok")
        b_full = sem("m_b_full"); c_full = sem("m_c_full"); dA_ok = sem("m_dA_ok"); dB_ok = sem("m_dB_ok")
        h_ok = sem("m_h_ok"); pr_ok = sem("m_pr_ok"); pr_used = sem("m_pr_used")
        cs_ok = sem("m_c_copied"); pp_ok = sem("m_pool_product_ok")
        y_ok = sem("m_y_ok"); yg_ok = sem("m_yg_ok"); o_full = sem("m_o_full"); o_ok = sem("m_o_ok")

        READ = {("bc",): (bc_split, 5, 2)}
        for m in range(KI):
            READ["in", m] = (xi_ok, KI, m + 1)
            READ["in", KI + m] = (z_ok, KI, m + 1)
            READ["dt", m] = (dt_ok, KI + 2, m + 1)

        def slot(*job):
            return W[ring.of[job][0]]

        def wait_full(e, b, *job):
            s, use = ring.of[job]
            e.wait_ge(full[s], b * ring.uses[s] + use + 1)

        def wait_slot(e, b, *job):
            at = JOBS_M.index(job)
            if at >= 3:
                s, per, k = READ[JOBS_M[at - 3]]
                e.wait_ge(s, b * per + k)

        LOADS = 13
        with nc.Block() as block:
            @block.sync
            def _(sp):
                def load(dst, src):
                    sp.dma_start(dst, src).then_inc(w_ok, 16)

                load(w_in[:, :, :], g["W_inT"].rearrange("(k p) n -> p k n", p=P))
                with nc.allow_non_contiguous_dma(reason="small weights, once"):
                    for i in range(3):
                        load(w_bc[:, :, 2 * NS * i:2 * NS * (i + 1)], g["W_xprojT"][:, DR:].rearrange("(k p) n -> p k n", p=P))
                    load(w_bc[:, :, 6 * NS:], g["W_xprojT"][:, 0:DR].rearrange("(k p) n -> p k n", p=P))
                    load(w_dt[:, :], g["W_dtT"])
                    load(w_out[:, :, :], g["W_outT"].rearrange("(k p) n -> p k n", p=P))
                    load(acol[:, :, :], g["A_log"].rearrange("(k p) n -> p k n", p=P))
                    load(taps[:, :, :], g["conv_w"].rearrange("(k p) n -> p k n", p=P))
                    for i, n in enumerate(("conv_b", "b_dt", "D_skip")):
                        load(vecs[:, i, :], g[n].rearrange("(k p) -> p k", p=P))
                    load(ident[:, :], g["ident"])
                sp.dma_start(xT[:, :, :], g["xn1T_s"][0]).then_inc(x_in, 16)

                def batch(b, last):
                    if not last:
                        sp.wait_ge(z_ok, b * KI + KI)
                        sp.dma_start(xT[:, :, :], g["xn1T_s"][b + 1]).then_inc(x_in, 16)
                    sp.wait_ge(o_ok, b * 2 + 2)
                    sp.dma_start(g["m_s"][b].rearrange("(t p) d -> p t d", p=P), so[:, :, :]).then_inc(stored, 16)

                with sp.Fori(0, B - 1) as b:
                    batch(b, False)
                batch(B - 1, True)
                sp.wait_ge(stored, 16 * B)

            @block.gpsimd
            def _(pool):
                nc.gpsimd.memset(xi[:, :, 0:DC - 1], 0.0).then_inc(prep, 1)
                nc.gpsimd.memset(one[:, :], 1.0).then_inc(prep, 1)
                nc.gpsimd.memset(pick[:, :, :], 0.0).then_inc(prep, 1)
                for i in range(3):
                    pool.wait_ge(prep, 3 + i)
                    nc.gpsimd.affine_select(out=pick[:, :, :], in_=pick[:, :, :], compare_op=ALU.not_equal, fill=1.0, base=-2 * NS * i,
                                            pattern=[[-1, 2 * NS], [0, P]], channel_multiplier=1).then_inc(prep, 1)
                with pool.Fori(0, B) as b:
                    for m in range(KI):
                        pool.wait_ge(dt_ok, b * (KI + 2) + KI + m // 2 + 1)
                        nc.gpsimd.tensor_tensor(du[:, m * L:(m + 1) * L], dt[:, m * L:(m + 1) * L], u[:, m * L:(m + 1) * L],
                                                ALU.mult).then_inc(du_ok, 1)
                    with pool.Fori(0, KI) as m:
                        n = b * KI + m
                        for k in range(NO):
                            s = 2 * k + 1
                            pool.wait_ge(cs_ok, n * NO + k + 2)
                            pool.wait_ge(pr_used, n * NS + s + 1)
                            pool.wait_ge(h_ok, n * NS + s + 3)
                            nc.gpsimd.tensor_tensor(pr[:, 1, :], h[:, 1, :], csb[k % 2][:, :], ALU.mult).then_inc(pp_ok, 1)

            @block.scalar
            def _(ac):
                A = nc.scalar.activation
                ac.wait_ge(w_ok, 16 * LOADS)
                ac.wait_ge(prep, 6)
                A(acol[:, :, :], acol[:, :, :], ACT.Exp).then_inc(prep, 1)
                ac.wait_ge(prep, 8)
                with ac.Fori(0, B) as b:
                    for m in range(KI):
                        wait_full(ac, b, "in", m)
                        A(xi[:, m, DC - 1:], slot("in", m)[:, :], ACT.Identity).then_inc(xi_ok, 1)
                    def gate_in(m):
                        wait_full(ac, b, "in", KI + m)
                        A(zs[:, m * L:(m + 1) * L], slot("in", KI + m)[:, :], ACT.Silu).then_inc(z_ok, 1)

                    def conv_out(m):
                        ac.wait_ge(conv_ok, b * KI + m + 1)
                        A(u[:, m * L:(m + 1) * L], u[:, m * L:(m + 1) * L], ACT.Silu).then_inc(u_ok, 1)

                    for m in range(KI):
                        conv_out(m)
                        gate_in(m)
                    wait_full(ac, b, "bc")
                    A(dr[:, :], slot("bc")[6 * NS:6 * NS + DR, :], ACT.Identity).then_inc(dr_ok, 1)
                    for m in range(KI):
                        wait_full(ac, b, "dt", m)
                        A(soft[m // 2][:, m % 2, :], slot("dt", m)[:, :], ACT.Abs, bias=vecs[:, 1, m:m + 1]).then_inc(soft_ok, 1)
                    for i in range(2):
                        ac.wait_ge(soft_ok, b * 6 + 2 * i + 2)
                        A(soft[i][:, :, :], soft[i][:, :, :], ACT.Exp, scale=-1.0).then_inc(soft_ok, 1)
                    for i in range(2):
                        ac.wait_ge(soft_ok, b * 6 + 5 + i)
                        A(soft[i][:, :, :], soft[i][:, :, :], ACT.Ln, bias=one[:, :]).then_inc(log_ok, 1)
                    ac.wait_ge(dt_ok, b * (KI + 2) + KI + 2)
                    with ac.Fori(0, KI) as m:
                        n = b * KI + m
                        for s in range(NS):
                            ac.wait_ge(h_ok, n * NS + s + 1)
                            A(dA[:, s % 2, :], dt[:, bass.ds(m * L, L)], ACT.Exp, scale=acol[:, bass.ds(m, 1), s]).then_inc(dA_ok, 1)
                            if s % 2:
                                k = s // 2
                                ac.wait_ge(c_full, n * NS + s + 1)
                                ac.wait_ge(pp_ok, n * NO + k + 1)
                                A(csb[k % 2][:, :], c_slot(s)[:, :], ACT.Identity).then_inc(cs_ok, 1)

            @block.vector
            def _(dv):
                v_ = nc.vector
                dv.wait_ge(prep, 7)
                v_.tensor_scalar(acol[:, :, :], acol[:, :, :], -1.0, None, ALU.mult).then_inc(prep, 1)
                v_.memset(h[:, 0, 0:1], 0.0).then_inc(y_ok, 1)
                dv.wait_ge(y_ok, 1)
                v_.memset(dB[:, 0, 0:1], 0.0).then_inc(dB_ok, 1)
                v_.memset(pr[:, 0, 0:1], 0.0).then_inc(pr_ok, 1)
                v_.memset(pr[:, 1, 0:1], 0.0).then_inc(pp_ok, 2)
                v_.memset(dA[:, 0, 0:1], 0.0).then_inc(cs_ok, 1)
                dv.wait_ge(dB_ok, 1)
                v_.memset(h[:, 1, 0:1], 0.0).then_inc(pr_used, 2)
                dv.wait_ge(pr_used, 2)
                dv.wait_ge(pr_ok, 1)
                dv.wait_ge(pp_ok, 2)
                dv.wait_ge(cs_ok, 1)
                for i in range(2):
                    v_.memset(h[:, i, 1:2], 0.0).then_inc(h_ok, 1)
                with dv.Fori(0, B) as b:
                    n_ = [0]

                    def link(k):
                        n_[0] += k
                        dv.wait_ge(chain, b * 3 * KI + n_[0])

                    for m in range(KI):
                        um = u[:, m * L:(m + 1) * L]
                        dv.wait_ge(xi_ok, b * KI + m + 1)
                        v_.tensor_scalar(um, xi[:, m, 0:L], taps[:, m, 0:1], vecs[:, 0, m:m + 1], ALU.mult, ALU.add).then_inc(chain, 1)
                        link(1)
                        for k in range(1, DC):
                            i = v_.scalar_tensor_tensor(um, xi[:, m, k:k + L], taps[:, m, k:k + 1], um, ALU.mult, ALU.add)
                            if k < DC - 1:
                                i.then_inc(chain, 1)
                                link(1)
                            else:
                                i.then_inc(conv_ok, 1)
                    wait_full(dv, b, "bc")
                    v_.tensor_copy(bcs[:, :], slot("bc")[0:96, :]).then_inc(bc_split, 1)
                    dv.wait_ge(bc_split, b * 5 + 1)
                    v_.tensor_tensor(bcr[:, :], slot("bc")[0:96, :], bcs[:, :], ALU.subtract).then_inc(bc_split, 1)
                    dv.wait_ge(bc_split, b * 5 + 2)
                    v_.tensor_copy(bc2[:, :], bcr[:, :]).then_inc(bc_split, 1)
                    dv.wait_ge(bc_split, b * 5 + 3)
                    v_.tensor_tensor(bcr[:, :], bcr[:, :], bc2[:, :], ALU.subtract).then_inc(bc_split, 1)
                    v_.tensor_copy(bcs[32:64, :], bc2[32:64, :]).then_inc(bc_split, 1)
                    dv.wait_ge(bc_split, b * 5 + 5)
                    v_.tensor_copy(bcs[64:96, :], bcr[64:96, :]).then_inc(bcs_ok, 1)
                    for m in range(KI):
                        dv.wait_ge(soft_ok, b * 6 + m + 1)
                        v_.tensor_scalar(dt[:, m * L:(m + 1) * L], slot("dt", m)[:, :], vecs[:, 1, m:m + 1], 0.0,
                                         ALU.add, ALU.max).then_inc(dt_ok, 1)
                    for i in range(2):
                        both = dt[:, 2 * i * L:2 * (i + 1) * L]
                        dv.wait_ge(dt_ok, b * (KI + 2) + KI)
                        dv.wait_ge(log_ok, b * 2 + i + 1)
                        v_.tensor_tensor(both, both, soft[i][:, :, :].rearrange("p s t -> p (s t)"), ALU.add).then_inc(dt_ok, 1)

                    def times_b(m, s):
                        n = b * KI + m
                        dv.wait_ge(b_full, n * NS + s + 1)
                        v_.tensor_tensor(dB[:, s % 2, :], du[:, bass.ds(m * L, L)], b_slot(s)[:, :], ALU.mult).then_inc(dB_ok, 1)

                    def gate(m):
                        n = b * KI + m
                        dv.wait_ge(pr_used, n * NS + NS + 2)
                        v_.scalar_tensor_tensor(yT[:, bass.ds(m * L, L)], u[:, bass.ds(m * L, L)], vecs[:, 2, bass.ds(m, 1)], Y[:, :],
                                                ALU.mult, ALU.add).then_inc(y_ok, 1)
                        dv.wait_ge(y_ok, n + 2)
                        v_.tensor_tensor(yT[:, bass.ds(m * L, L)], yT[:, bass.ds(m * L, L)], zs[:, bass.ds(m * L, L)], ALU.mult).then_inc(yg_ok, 1)

                    def tile(m, first):
                        n = b * KI + m
                        if first:
                            dv.wait_ge(dt_ok, b * (KI + 2) + KI + 2)
                        dv.wait_ge(du_ok, n + 1)
                        times_b(m, 0)
                        for s in range(NS):
                            dv.wait_ge(dB_ok, n * NS + s + 2)
                            dv.wait_ge(dA_ok, n * NS + s + 1)
                            if s % 2:
                                dv.wait_ge(pp_ok, n * NO + s // 2 + 2)
                            v_.tensor_tensor_scan(h[:, s % 2, :], dA[:, s % 2, :], dB[:, s % 2, :], 0.0, ALU.mult, ALU.add).then_inc(h_ok, 1)
                            if s < NS - 1:
                                times_b(m, s + 1)
                            if s == 1 and not first:
                                gate(m - 1)
                            if s % 2:
                                continue
                            dv.wait_ge(h_ok, n * NS + s + 3)
                            dv.wait_ge(c_full, n * NS + s + 1)
                            dv.wait_ge(pr_used, n * NS + s + 1)
                            v_.tensor_tensor(pr[:, 0, :], h[:, 0, :], c_slot(s)[:, :], ALU.mult).then_inc(pr_ok, 1)

                    tile(0, True)
                    with dv.Fori(1, KI) as m:
                        tile(m, False)
                    gate(KI - 1)
                    for i, o in enumerate((X, Y)):
                        dv.wait_ge(o_full, b * 2 + i + 1)
                        if i == 0:
                            dv.wait_ge(z_ok, b * KI + KI)
                        v_.tensor_copy(so[:, 4 * i:4 * i + 4, :].rearrange("p t d -> p (t d)"), o[:, :]).then_inc(o_ok, 1)
                    dv.wait_ge(stored, b * 16 + 16)

            @block.tensor
            def _(pe):
                mm = nc.tensor.matmul
                pe.wait_ge(w_ok, 16 * LOADS)
                pe.wait_ge(prep, 6)

                def done(ins, *job):
                    ins.then_inc(full[ring.of[job][0]], 1)

                with pe.Fori(0, B) as b:
                    pe.wait_ge(x_in, b * 16 + 16)
                    for j in range(2 * KI):
                        wait_slot(pe, b, "in", j)
                        for c in range(NC_):
                            for k in range(KD):
                                ins = mm(slot("in", j)[:, c * CH:(c + 1) * CH], w_in[:, k, j * P:(j + 1) * P], xT[:, k, c * CH:(c + 1) * CH],
                                         start=(k == 0), stop=(k == KD - 1))
                        done(ins, "in", j)
                    pe.wait_ge(u_ok, b * KI + KI)
                    wait_slot(pe, b, "bc")
                    for c in range(NC_):
                        for k in range(KI):
                            ins = mm(slot("bc")[0:6 * NS + DR, c * CH:(c + 1) * CH], w_bc[:, k, :], u[:, k * L + c * CH:k * L + (c + 1) * CH],
                                     start=(k == 0), stop=(k == KI - 1))
                    done(ins, "bc")
                    pe.wait_ge(dr_ok, b + 1)
                    for m in range(KI):
                        wait_slot(pe, b, "dt", m)
                        for c in range(NC_):
                            ins = mm(slot("dt", m)[:, c * CH:(c + 1) * CH], w_dt[:, m * P:(m + 1) * P], dr[:, c * CH:(c + 1) * CH],
                                     start=True, stop=True)
                        done(ins, "dt", m)
                    def spread(dst, row, ok):
                        for c in range(NC_):
                            ins = mm(dst[:, c * CH:(c + 1) * CH], pick[:, row, :], bcs[:, c * CH:(c + 1) * CH], start=True, stop=True)
                        ins.then_inc(ok, 1)

                    def add_state(n, s):
                        if s == 0:
                            pe.wait_ge(y_ok, n + 1)
                        if s % 2:
                            pe.wait_ge(pp_ok, n * NO + s // 2 + 3)
                        else:
                            pe.wait_ge(pr_ok, n * NO + s // 2 + 2)
                        for c in range(NC_):
                            ins = mm(Y[:, c * CH:(c + 1) * CH], ident[:, :], pr[:, s % 2, c * CH:(c + 1) * CH],
                                     start=(s == 0), stop=(s == NS - 1), skip_group_check=True)
                        ins.then_inc(pr_used, 1)

                    def tile(m, first):
                        n = b * KI + m
                        if first:
                            pe.wait_ge(bcs_ok, b + 1)
                            pe.wait_ge(dt_ok, b * (KI + 2) + KI)
                        pe.wait_ge(dB_ok, n * NS + 1)
                        spread(b_slot(0), 0, b_full)
                        pe.wait_ge(cs_ok, n * NO + 1)
                        spread(c_slot(0), NS, c_full)
                        pe.wait_ge(pr_ok, n * NO + 1)
                        for s in range(NS):
                            if s < NS - 1:
                                if s % 2:
                                    pe.wait_ge(pr_ok, n * NO + (s - 1) // 2 + 2)
                                elif s:
                                    pe.wait_ge(cs_ok, n * NO + (s - 2) // 2 + 2)
                                spread(b_slot(s + 1), s + 1, b_full)
                                pe.wait_ge(dB_ok, n * NS + s + 2)
                                spread(c_slot(s + 1), NS + s + 1, c_full)
                            if s:
                                add_state(n, s - 1)
                            elif not first:
                                add_state(n - 1, NS - 1)

                    tile(0, True)
                    with pe.Fori(1, KI) as m:
                        tile(m, False)
                    add_state(b * KI + KI - 1, NS - 1)
                    pe.wait_ge(yg_ok, b * KI + KI)
                    for i, o in enumerate((X, Y)):
                        for t in range(4):
                            for k in range(KI):
                                at = k * L + (4 * i + t) * P
                                ins = mm(o[:, t * D:(t + 1) * D], yT[:, at:at + P], w_out[:, k, :], start=(k == 0), stop=(k == KI - 1))
                        ins.then_inc(o_full, 1)
                    pe.wait_ge(o_ok, b * 2 + 2)


NTILE = 40
S = NTILE * P
GROUP = 4
N1, N2 = E * HE // P, E * D // P


def phase_e(nc, g):
    with ExitStack() as ctx:
        def sb(name, shape, dt=F32):
            return ctx.enter_context(nc.sbuf_tensor(name, shape, dt))

        def sem(name):
            return ctx.enter_context(nc.semaphore(name))

        def ps(name, shape):
            return ctx.enter_context(nc.psum_tensor(name, shape, F32))

        lg = g["lg"]
        one_hot_at = []
        e_w1 = sb("e_w1", [P, KD, E * HE])
        e_w2 = sb("e_w2", [P, HE // P, E * D])
        brow = sb("e_brow", [P, (N1 + N2)])
        brs = sb("e_brs", [P, (N1 + N2)])
        bsp = sb("e_bsp", [P, 3, (N1 + N2)], BF16)
        bias3 = sb("e_bias3", [3, E * (HE + D)], BF16)
        ones3 = sb("e_ones3", [3, P], BF16)
        ident = sb("ident_e", [P, P])
        tri = sb("tri", [P, P])
        ones = sb("ones_e", [P, P])
        part = sb("part", [P, NT, D])
        taken = [0]

        def table(t, e, by_tile=True):
            at = taken[0]
            taken[0] += t * e
            return part[:, :, :].rearrange("p t d -> p (t d)")[:, at:at + t * e].rearrange("p (a b) -> p a b", b=e if by_tile else t)

        eidx_i = sb("eidx_i", [P, NT, E], I32)
        eidx = table(NT, E)
        jidx_i = sb("jidx_i", [P, NTILE, E], I32)
        jidx = table(NTILE, E)
        keep = sb("keep", [P, E, NT])
        one8 = sb("one8", [P, E])
        gamma = sb("gamma", [P, 2, D])

        m8 = sb("m8", [P, NT]); ex = table(NT, E)
        srt = sb("srt", [P, NT, 8]); srti = sb("srti", [P, NT, 8], mybir.dt.uint32)
        idf = sb("idf", [P, NT, 2])
        oh = table(NT, E); tot = table(NT, E, False); inc = table(NT, E, False); a8 = table(NT, E)
        cnt = sb("cnt", [P, 4, E])
        jge = table(NTILE, E); jf = sb("jf", [P, NTILE])
        posf = sb("posf", [P, 1, NT]); pos = sb("pos", [P, 2, NT], I32)
        texp = sb("texp", [P, 2, NTILE], I32)

        spare = sb("e_spare", [P, 24])
        tok = sb("tok", [P, NT, D])
        got = sb("got", [P, NT, D])
        xs = sb("xs", [P, GROUP, D]); xsT = sb("xsT", [P, 2, KD * P]); hs = sb("hs", [P, 2, HE])
        hT = sb("hT", [P, 2, HE]); ys = sb("ys", [P, GROUP, D])
        st = sb("st_e", [P, NT, 6]); mv = sb("mv_e", [P, NT, 2]); rs = sb("rs_e", [P, 4, NT])
        pT1, pM1, pT2, pM2 = (ps(f"e_{n}", [P, 2, CH]) for n in ("T1", "M1", "T2", "M2"))
        X0, X1 = pT1[:, 0, :], pM1[:, 0, :]

        w_ok = sem("e_w_ok"); c_ok = sem("e_const"); bs = sem("e_bias_split"); b_in = sem("e_bias_in")
        rt = sem("e_route"); rt_pe = sem("e_route_pe"); rt_act = sem("e_route_act"); rt_ok = sem("e_route_ok")
        zeroed = sem("e_zeroed"); tok_in = [sem(f"e_tok_in{q}") for q in range(NT // GROUP)]; sc = sem("e_scattered")
        got_in = [sem(f"e_got_in{q}") for q in range(NT // GROUP)]; part_ok = sem("e_part_ok"); boosted = sem("e_boosted")
        xs_in = [sem(f"e_xs_in{i}") for i in range(GROUP)]; t1 = sem("e_t1"); t1c = sem("e_t1c"); m1 = sem("e_m1"); m1c = sem("e_m1c")
        t2 = sem("e_t2"); t2c = sem("e_t2c"); m2 = sem("e_m2"); m2c = sem("e_m2c"); ys_out = [sem(f"e_ys_out{i}") for i in range(GROUP)]
        m_in = [sem(f"e_m_in{i}") for i in range(2)]; x1_in = sem("e_x1_in"); f_dve = sem("e_norm_chain"); f_n = sem("e_normed")
        f_act = sem("e_silu_ok"); f_ok = sem("e_out_ok"); f_out = sem("e_out_stored")
        NQ = NT // GROUP
        NG = NTILE // GROUP
        LOADS = 5 + 2 * E
        tokens = lambda ap: ap.rearrange("(t p) d -> p t d", p=P)
        flat = lambda ap: ap.rearrange("p t d -> p (t d)")
        group = lambda q: slice(q * GROUP, (q + 1) * GROUP)
        xn1_q = g["xn1_s"].rearrange("b (c n) d -> (b c) n d", n=GROUP * P)
        x1_all = g["x1_s"].rearrange("b n d -> (b n) d")
        m_q = g["m_s"].rearrange("b (c n) d -> (b c) n d", n=GROUP * P)
        out_q = g["out"].rearrange("b (c n) d -> (b c) n d", n=GROUP * P)

        def pipeline(engine, r, first, second, third, fourth):
            first(r, 0, 0)
            second(r, 0, 0)
            first(r, 0, 1)

            def turn(q, last):
                for i in range(GROUP):
                    third(r, q, i)
                    if not (last and i == GROUP - 1):
                        second(r, q + (i + 1) // GROUP, (i + 1) % GROUP)
                    if not (last and i >= GROUP - 2):
                        first(r, q + (i + 2) // GROUP, (i + 2) % GROUP)
                    fourth(r, q, i)

            with engine.Fori(0, NG - 1) as q:
                turn(q, False)
            turn(NG - 1, True)

        mbuf = (xs, ys)
        with nc.Block() as block:
            @block.sync
            def _(sp):
                def load(dst, src):
                    sp.dma_start(dst, src).then_inc(w_ok, 16)

                load(brow[:, 0:N1], g["e_b1"].rearrange("e n -> (e n)").rearrange("(p n) -> p n", p=P))
                load(brow[:, N1:], g["e_b2"].rearrange("e n -> (e n)").rearrange("(p n) -> p n", p=P))
                load(ident[:, :], g["ident"])
                for i, n in enumerate(("ln_gamma", "ln_beta")):
                    load(gamma[:, i, :], g[n].rearrange("(a n) -> a n", a=1).to_broadcast([P, D]))
                for q in range(NQ):
                    sp.dma_start(tok[:, group(q), :], tokens(xn1_q[q])).then_inc(tok_in[q], 16)
                sp.wait_ge(c_ok, 1)
                sp.dma_start(tokens(g["xs_s"]), xs[:, 0, :].unsqueeze(1).to_broadcast([P, NTILE, D])).then_inc(zeroed, 16)
                for e in range(E):
                    load(e_w1[:, :, e * HE:(e + 1) * HE], g["e_W1"][e].rearrange("(k p) n -> p k n", p=P))
                    load(e_w2[:, :, e * D:(e + 1) * D], g["e_W2"][e].rearrange("(k p) n -> p k n", p=P))
                sp.wait_ge(bs, 5)
                for i in range(3):
                    for at, a, n in ((0, 0, N1), (E * HE, N1, N2)):
                        sp.dma_start(bias3[i:i + 1, at:at + P * n].rearrange("a (p n) -> a p n", n=n), bsp[:, i, a:a + n]).then_inc(b_in, 16)
                for r in range(2):
                    sp.wait_ge(sc, (r + 1) * NT * 16)

                    def load_xs(q, i):
                        sp.wait_ge(t1, (r * NG + q) * GROUP + i + 1)
                        sp.dma_start(xs[:, i, :], g["xs_s"][bass.ds((q * GROUP + i) * P, P), :]).then_inc(xs_in[i], 16)

                    def turn(q, last):
                        for i in range(GROUP):
                            n = (r * NG + q) * GROUP + i
                            sp.wait_ge(m2c, n + 3)
                            sp.dma_start(g[f"y{r}_s"][bass.ds((q * GROUP + i) * P, P), :], ys[:, i, :]).then_inc(ys_out[i], 16)
                            if not last:
                                load_xs(q + 1, i)

                    for i in range(GROUP):
                        load_xs(0, i)
                    with sp.Fori(0, NG - 1) as q:
                        turn(q, False)
                    turn(NG - 1, True)
                sp.dma_start(tok[:, :, :], tokens(x1_all)).then_inc(x1_in, 16)

                def load_m(q):
                    sp.dma_start(mbuf[q % 2][:, :, :], tokens(m_q[q])).then_inc(m_in[q % 2], 16)

                for i in range(GROUP):
                    sp.wait_ge(ys_out[i], 16 * 2 * NG + 16)
                load_m(0)
                load_m(1)
                for q in range(NQ):
                    sp.wait_ge(f_ok, 2 * q + 2)
                    sp.dma_start(tokens(out_q[q]), got[:, group(q), :]).then_inc(f_out, 16)
                    if q + 2 < NQ:
                        load_m(q + 2)
                sp.wait_ge(f_out, NQ * 16)

            @block.gpsimd
            def _(pool):
                nc.gpsimd.memset(xs[:, 0, :], 0.0).then_inc(c_ok, 1)
                nc.gpsimd.memset(ones[:, :], 1.0).then_inc(c_ok, 1)
                nc.gpsimd.memset(one8[:, :], 1.0).then_inc(c_ok, 1)
                nc.gpsimd.memset(ones3[:, :], 1.0).then_inc(c_ok, 1)
                nc.gpsimd.memset(keep[:, :, :], 1.0).then_inc(c_ok, 1)
                nc.gpsimd.iota(eidx_i[:, :, :], pattern=[[0, NT], [1, E]], base=0, channel_multiplier=0).then_inc(c_ok, 1)
                nc.gpsimd.iota(jidx_i[:, :, :], pattern=[[1, NTILE], [0, E]], base=0, channel_multiplier=0).then_inc(c_ok, 1)
                pool.wait_ge(c_ok, 7)
                nc.gpsimd.memset(keep[:, :, 0:1], 0.0).then_inc(c_ok, 1)
                nc.gpsimd.affine_select(out=tri[:, :], in_=ones[:, :], compare_op=ALU.is_gt, fill=0.0, base=0,
                                        pattern=[[1, P]], channel_multiplier=-1).then_inc(c_ok, 1)
                pool.wait_ge(rt_ok, 1)
                pool.wait_ge(zeroed, 16)

                def rows(table, t, r):
                    return table, bass.IndirectOffsetOnAxis(ap=pos[:, r, t:t + 1], axis=0)

                def gather(r):
                    for i in range(GROUP):
                        pool.wait_ge(ys_out[i], 16 * NG * (r + 1) + 16)
                    for q in range(NQ):
                        if r:
                            pool.wait_ge(part_ok, GROUP * (q + 1))
                            pool.wait_ge(boosted, q + 1)
                        for t in range(q * GROUP, (q + 1) * GROUP):
                            nc.gpsimd.indirect_dma_start(got[:, t, :], None, *rows(g[f"y{r}_s"], t, r)).then_inc(got_in[q], 16)

                for q in range(NQ):
                    pool.wait_ge(tok_in[q], 16)
                    for t in range(q * GROUP, (q + 1) * GROUP):
                        nc.gpsimd.indirect_dma_start(*rows(g["xs_s"], t, 0), tok[:, t, :], None).then_inc(sc, 16)
                gather(0)
                for q in range(NQ):
                    pool.wait_ge(boosted, q + 1)
                    for t in range(q * GROUP, (q + 1) * GROUP):
                        nc.gpsimd.indirect_dma_start(*rows(g["xs_s"], t, 1), tok[:, t, :], None).then_inc(sc, 16)
                gather(1)

            @block.scalar
            def _(ac):
                A = nc.scalar.activation
                ac.wait_ge(rt, 2)
                A(ex[:, :, :], ex[:, :, :], ACT.Exp).then_inc(rt_act, 1)
                def turned_in(r, q, i):
                    n = (r * NG + q) * GROUP + i
                    ac.wait_ge(t1, n + GROUP + 1)
                    ac.wait_ge(m1, n + 1)
                    A(xsT[:, i % 2, :], pT1[:, i % 2, 0:KD * P], ACT.Identity).then_inc(t1c, 1)

                def hidden(r, q, i):
                    n = (r * NG + q) * GROUP + i
                    ac.wait_ge(m1, n + 3)
                    ac.wait_ge(t2, n + 1)
                    A(hs[:, i % 2, :], pM1[:, i % 2, :], ACT.Relu).then_inc(m1c, 1)

                def hidden_turned(r, q, i):
                    n = (r * NG + q) * GROUP + i
                    ac.wait_ge(t2, n + 3)
                    ac.wait_ge(m2, n + 1)
                    A(hT[:, i % 2, :], pT2[:, i % 2, :], ACT.Identity).then_inc(t2c, 1)

                def rows_out(r, q, i):
                    n = (r * NG + q) * GROUP + i
                    ac.wait_ge(m2, n + 3)
                    ac.wait_ge(ys_out[i], 16 * (r * NG + q) + 16)
                    A(ys[:, i, :], pM2[:, i % 2, 0:D], ACT.Identity).then_inc(m2c, 1)

                for r in range(2):
                    pipeline(ac, r, turned_in, hidden, hidden_turned, rows_out)
                for q in range(NQ):
                    ac.wait_ge(f_n, q + 1)
                    A(got[:, group(q), :], got[:, group(q), :], ACT.Silu).then_inc(f_act, 1)

            @block.vector
            def _(dv):
                v_ = nc.vector
                k = [0]

                def step(ins):
                    ins.then_inc(rt, 1)
                    k[0] += 1
                    dv.wait_ge(rt, k[0])

                over_e = lambda ap, n: ap.unsqueeze(2).to_broadcast([P, n, E])
                over_t = lambda ap, n: ap.unsqueeze(1).to_broadcast([P, n, E])
                step(v_.tensor_reduce(m8[:, :], lg[:, :, :], AX.X, ALU.max))
                step(v_.tensor_tensor(ex[:, :, :], lg[:, :, :], over_e(m8[:, :], NT), ALU.subtract))
                dv.wait_ge(rt_act, 1)
                step(v_.tensor_reduce(m8[:, :], ex[:, :, :], AX.X, ALU.add))
                step(v_.reciprocal(m8[:, :], m8[:, :]))
                step(v_.tensor_tensor(ex[:, :, :], ex[:, :, :], over_e(m8[:, :], NT), ALU.mult))
                for t in range(NT):
                    v_.max(srt[:, t, :], ex[:, t, :]).then_inc(rt, 1)
                k[0] += NT
                dv.wait_ge(rt, k[0])
                for t in range(NT):
                    v_.max_index(srti[:, t, :], srt[:, t, :], ex[:, t, :]).then_inc(rt, 1)
                k[0] += NT
                dv.wait_ge(rt, k[0])
                step(v_.tensor_copy(idf[:, :, :], srti[:, :, 0:2]))
                dv.wait_ge(c_ok, 9)
                step(v_.tensor_copy(eidx[:, :, :], eidx_i[:, :, :]))
                step(v_.tensor_copy(jidx[:, :, :], jidx_i[:, :, :]))
                for r in range(2):
                    step(v_.tensor_tensor(oh[:, :, :], eidx[:, :, :], over_e(idf[:, :, r], NT), ALU.is_equal))
                    one_hot_at.append(k[0])
                    dv.wait_ge(rt_pe, 2 * r + 2)
                    step(v_.tensor_copy(tot[:, :, :], X1[:, 0:NT * E].rearrange("p (t e) -> p e t", e=E)))
                    flat = lambda ap: ap.rearrange("p e t -> p (e t)")
                    step(v_.tensor_tensor_scan(flat(inc[:, :, :]), flat(keep[:, :, :]), flat(tot[:, :, :]), 0.0, ALU.mult, ALU.add))
                    step(v_.tensor_tensor(tot[:, :, :], inc[:, :, :], tot[:, :, :], ALU.subtract))
                    step(v_.tensor_scalar(cnt[:, 0, :], inc[:, :, NT - 1], 1.0 / P, (P / 2 - 0.5) / P, ALU.mult, ALU.add))
                    step(v_.tensor_scalar(cnt[:, 0, :], cnt[:, 0, :], ROUND, ROUND, ALU.add, ALU.subtract))
                    step(v_.tensor_tensor_scan(cnt[:, 1, :], one8[:, :], cnt[:, 0, :], 0.0, ALU.mult, ALU.add))
                    step(v_.tensor_tensor(cnt[:, 2, :], cnt[:, 1, :], cnt[:, 0, :], ALU.subtract))
                    step(v_.tensor_scalar(cnt[:, 2, :], cnt[:, 2, :], float(P), None, ALU.mult))
                    step(v_.tensor_tensor(a8[:, :, :], X0[:, 0:NT * E].rearrange("p (t e) -> p t e", e=E),
                                          tot[:, :, :].rearrange("p e t -> p t e"), ALU.add))
                    step(v_.tensor_tensor(a8[:, :, :], a8[:, :, :], over_t(cnt[:, 2, :], NT), ALU.add))
                    step(v_.tensor_tensor(a8[:, :, :], a8[:, :, :], oh[:, :, :], ALU.mult))
                    step(v_.tensor_reduce(posf[:, 0, :], a8[:, :, :], AX.X, ALU.add))
                    step(v_.tensor_copy(pos[:, r, :], posf[:, 0, :]))
                    step(v_.tensor_tensor(jge[:, :, :], jidx[:, :, :], over_t(cnt[:, 1, :], NTILE), ALU.is_ge))
                    step(v_.tensor_reduce(jf[:, :], jge[:, :, :], AX.X, ALU.add))
                    step(v_.tensor_scalar(jf[:, :], jf[:, :], float(E - 1), None, ALU.min))
                    step(v_.tensor_copy(texp[:, r, :], jf[:, :]))
                for i, (s, n) in enumerate(((t1, GROUP), (t1c, 2), (m1, 2), (m1c, 2), (t2, 2), (t2c, 2), (m2, 2), (m2c, 2), (rt_ok, 1))
                                           + tuple((s, 16) for s in ys_out)):
                    v_.memset(spare[:, i:i + 1], 0.0).then_inc(s, n)
                dv.wait_ge(w_ok, 16 * LOADS)
                for i in range(3):
                    src = brs if i else brow
                    v_.tensor_copy(bsp[:, i, :], src[:, :]).then_inc(bs, 1)
                    if i < 2:
                        dv.wait_ge(bs, 2 * i + 1)
                        v_.tensor_tensor(brs[:, :], src[:, :], bsp[:, i, :], ALU.subtract).then_inc(bs, 1)
                        dv.wait_ge(bs, 2 * i + 2)
                for q in range(NQ):
                    dv.wait_ge(got_in[q], GROUP * 16)
                    for t in range(q * GROUP, (q + 1) * GROUP):
                        v_.scalar_tensor_tensor(part[:, t, :], got[:, t, :], srt[:, t, 0:1], tok[:, t, :], ALU.mult, ALU.add).then_inc(part_ok, 1)
                    dv.wait_ge(part_ok, GROUP * (q + 1))
                    if not q:
                        dv.wait_ge(sc, NT * 16)
                    v_.scalar_tensor_tensor(flat(tok[:, group(q), :]), flat(got[:, group(q), :]), 0.5, flat(tok[:, group(q), :]),
                                            ALU.mult, ALU.add).then_inc(boosted, 1)
                c = [0]

                def link(ins, n=1):
                    ins.then_inc(f_dve, 1)
                    c[0] += 1
                    if n:
                        dv.wait_ge(f_dve, c[0])

                for q in range(NQ):
                    dv.wait_ge(got_in[q], 2 * GROUP * 16)
                    for t in range(q * GROUP, (q + 1) * GROUP):
                        link(v_.scalar_tensor_tensor(got[:, t, :], got[:, t, :], srt[:, t, 1:2], part[:, t, :], ALU.mult, ALU.add),
                             t % GROUP == GROUP - 1)
                    for t in range(q * GROUP, (q + 1) * GROUP):
                        link(v_.bn_stats(st[:, t, :], got[:, t, :]), t % GROUP == GROUP - 1)
                    for t in range(q * GROUP, (q + 1) * GROUP):
                        link(v_.bn_aggr(mv[:, t, :], st[:, t, :]), t == NT - 1)
                var, y, y2, hh = (rs[:, i, :] for i in range(4))
                link(v_.tensor_scalar(var, mv[:, :, 1], EPS, None, ALU.add))
                link(v_.tensor_scalar(hh.bitcast(I32), var.bitcast(I32), 1, None, ALU.logical_shift_right))
                link(v_.tensor_scalar(y.bitcast(I32), hh.bitcast(I32), -1.0, RSQRT_SEED, ALU.mult, ALU.add))
                for _ in range(4):
                    link(v_.tensor_tensor(y2, y, y, ALU.mult))
                    link(v_.tensor_tensor(y2, y2, var, ALU.mult))
                    link(v_.tensor_scalar(y2, y2, -0.5, 1.5, ALU.mult, ALU.add))
                    link(v_.tensor_tensor(y, y, y2, ALU.mult))
                gb = lambda i: gamma[:, i, :].unsqueeze(1).to_broadcast([P, GROUP, D])

                def gated(q):
                    dv.wait_ge(f_act, q + 1)
                    dv.wait_ge(m_in[q % 2], 16 * (q // 2) + 16)
                    v_.tensor_tensor(got[:, group(q), :], got[:, group(q), :], mbuf[q % 2][:, :, :], ALU.mult).then_inc(f_ok, 1)
                    dv.wait_ge(f_ok, 2 * q + 1)
                    if not q:
                        dv.wait_ge(x1_in, 16)
                    v_.tensor_tensor(got[:, group(q), :], got[:, group(q), :], tok[:, group(q), :], ALU.add).then_inc(f_ok, 1)

                for q in range(NQ):
                    for t in range(q * GROUP, (q + 1) * GROUP):
                        link(v_.tensor_scalar(got[:, t, :], got[:, t, :], mv[:, t, 0:1], y[:, t:t + 1], ALU.subtract, ALU.mult),
                             t % GROUP == GROUP - 1)
                    link(v_.tensor_tensor(got[:, group(q), :], got[:, group(q), :], gb(0), ALU.mult))
                    v_.tensor_tensor(got[:, group(q), :], got[:, group(q), :], gb(1), ALU.add).then_inc(f_n, 1)
                    if q:
                        gated(q - 1)
                gated(NQ - 1)

            @block.tensor
            def _(pe):
                mm = nc.tensor.matmul
                pe.wait_ge(c_ok, 9)
                for r in range(2):
                    pe.wait_ge(rt, one_hot_at[r])
                    flat = oh[:, :, :].rearrange("p t e -> p (t e)")
                    mm(X0[:, 0:NT * E], tri[:, :], flat, start=True, stop=True).then_inc(rt_pe, 1)
                    mm(X1[:, 0:NT * E], ones[:, :], flat, start=True, stop=True).then_inc(rt_pe, 1)
                pe.wait_ge(rt_ok, 1)
                pe.wait_ge(b_in, 96)
                pe.wait_ge(w_ok, 16 * LOADS)
                def turned_in(r, q, i):
                    n = (r * NG + q) * GROUP + i
                    pe.wait_ge(xs_in[i], (r * NG + q) * 16 + 16)
                    pe.wait_ge(t1c, n + 1)
                    for k in range(KD):
                        ins = nc.tensor.transpose(pT1[:, i % 2, k * P:(k + 1) * P], xs[:, i, k * P:(k + 1) * P], ident[:, :])
                    ins.then_inc(t1, 1)

                def hidden(r, q, i):
                    n = (r * NG + q) * GROUP + i
                    e = pe.value_load(texp[0:1, r, bass.ds(q * GROUP + i, 1)], min_val=0, max_val=E - 1)
                    pe.wait_ge(t1c, n + 3)
                    pe.wait_ge(m1c, n + 1)
                    for k in range(KD):
                        mm(pM1[:, i % 2, :], xsT[:, i % 2, k * P:(k + 1) * P], e_w1[:, k, bass.ds(e * HE, HE)], start=(k == 0), stop=False)
                    mm(pM1[:, i % 2, :], ones3[:, :], bias3[:, bass.ds(e * HE, HE)], start=False, stop=True).then_inc(m1, 1)

                def hidden_turned(r, q, i):
                    n = (r * NG + q) * GROUP + i
                    pe.wait_ge(m1c, n + 3)
                    pe.wait_ge(t2c, n + 1)
                    for k in range(HE // P):
                        ins = nc.tensor.transpose(pT2[:, i % 2, k * P:(k + 1) * P], hs[:, i % 2, k * P:(k + 1) * P], ident[:, :])
                    ins.then_inc(t2, 1)

                def rows_out(r, q, i):
                    n = (r * NG + q) * GROUP + i
                    e = pe.value_load(texp[0:1, r, bass.ds(q * GROUP + i, 1)], min_val=0, max_val=E - 1)
                    pe.wait_ge(t2c, n + 3)
                    pe.wait_ge(m2c, n + 1)
                    for k in range(HE // P):
                        mm(pM2[:, i % 2, 0:D], hT[:, i % 2, k * P:(k + 1) * P], e_w2[:, k, bass.ds(e * D, D)], start=(k == 0), stop=False)
                    mm(pM2[:, i % 2, 0:D], ones3[:, :], bias3[:, bass.ds(e * D + E * HE, D)], start=False, stop=True).then_inc(m2, 1)

                for r in range(2):
                    pipeline(pe, r, turned_in, hidden, hidden_turned, rows_out)


def blocks(nc, g):
    for name, shape in (("x1_s", [B, L, D]), ("xn1_s", [B, L, D]), ("xn1T_s", [B, P, KD, L]), ("m_s", [B, L, D]),
                        ("xs_s", [S, D]), ("y0_s", [S, D]), ("y1_s", [S, D]), ("part_s", [NT // 4, 4 * P, D])):
        g[name] = nc.dram_tensor(name, shape, F32).ap()
    with nc.sbuf_tensor("lg", [P, NT, E], F32) as lg:
        g["lg"] = lg
        phase_a(nc, g)
        phase_m(nc, g)
        phase_e(nc, g)


INPUTS = (
    [(n, "L0_attn_" + n, False) for n in ("bq", "bk", "ln1_g", "ln1_b", "ln2_g", "ln2_b", "b1", "bv", "bo", "b2",
                                          "wq", "wk", "wv", "wo", "w1", "w2", "x")]
    + [("proj", "L0_attn_proj_mat", False), ("mu_r", "L0_ffn_mu_r", False), ("mu_k", "L0_ffn_mu_k", False)]
    + [(f"W_{n}T", "L0_ffn_W_" + n, True) for n in "rkv"]
    + [(n + "T", "L1_attn_" + n, True) for n in ("W_in", "W_xproj", "W_dt", "W_out")]
    + [(n, "L1_attn_" + n, False) for n in ("A_log", "conv_w", "conv_b", "b_dt", "D_skip")]
    + [(n, "L1_ffn_" + n, False) for n in ("gate_W", "gate_b", "ln_gamma", "ln_beta")]
    + [("e_" + n, "L1_ffn_" + n, False) for n in ("W1", "b1", "W2", "b2")]
)


def kernel(**inputs):
    import concourse.bacc as bacc
    from concourse.bass_utils import run_bass_kernel_spmd

    nc = bacc.Bacc("TRN2", target_bir_lowering=False, num_devices=1)
    arrays, g = {}, {}
    for name, source, transposed in INPUTS:
        a = np.asarray(inputs[source])
        arrays["in_" + name] = np.ascontiguousarray(a.T if transposed else a)
    arrays["in_ident"] = np.eye(P, dtype=np.float32)
    for name, a in arrays.items():
        g[name[3:]] = nc.dram_tensor(name, a.shape, F32, kind="ExternalInput").ap()
    g["out"] = nc.dram_tensor("out", [B, L, D], F32, kind="ExternalOutput").ap()
    blocks(nc, g)
    r = run_bass_kernel_spmd(nc, [arrays], core_ids=[0])
    return r.results[0]["out"]
```
